# Optimizing a Trainium2 kernel written in Bass

```python
import numpy as np
import jax
import jax.numpy as jnp

def _softmax(x, axis=-1):
    return jax.nn.softmax(x, axis=axis)

def _gelu(x):
    return jax.nn.gelu(x, approximate=True)

def _silu(x):
    return jax.nn.silu(x)

def _sigmoid(x):
    return jax.nn.sigmoid(x)

def _layernorm(x, axis=-1, eps=1e-05):
    m = jnp.mean(x, axis=axis, keepdims=True)
    v = jnp.var(x, axis=axis, keepdims=True)
    return (x - m) / jnp.sqrt(v + eps)

def _scatter_add(tgt, idx, src, axis=0):
    return tgt.at[idx].add(src)

def _segment_sum(src, seg, n):
    return jax.ops.segment_sum(src, seg, n)
kernel_name = 'mk_decoder_preln_d1_seqx_r4_880df7'

def setup_inputs(seed: int=0):
    np.random.seed(seed)
    _w = jnp.asarray

    def _rec_inputs():
        import jax
        import jax.numpy as jnp
        _rk = jax.random.key(seed)
        x = -0.0002928 + 1 * jax.random.normal(jax.random.fold_in(_rk, 1), (4, 1024, 256), jnp.float32)
        _lenS = 1024 - jax.random.randint(jax.random.fold_in(_rk, 7), (4,), 0, max(1, 1024 // 4) + 1, jnp.int32)
        _lenS2 = 64 - jax.random.randint(jax.random.fold_in(_rk, 8), (4,), 0, max(1, 64 // 4) + 1, jnp.int32)
        _ctx_1024P = jax.random.normal(jax.random.fold_in(_rk, 11), (4, 16, 256), jnp.float32)
        _ctx_1024c = jax.random.dirichlet(jax.random.fold_in(_rk, 511), 0.3 * jnp.ones((16,), jnp.float32), (4, 64))
        _ctx_1024t = jnp.einsum('bsk,bkd->bsd', _ctx_1024c, _ctx_1024P)
        _ctx_1024t = _ctx_1024t * jax.lax.rsqrt(jnp.mean(jnp.square(_ctx_1024t)) + 1e-12) * 0.953939
        ctx_1024 = -1.39393e-06 + 0.999914 * (_ctx_1024t + 0.3 * jax.random.normal(jax.random.fold_in(_rk, 611), (4, 64, 256), jnp.float32))
        return (x, ctx_1024)
    x, ctx_1024 = _rec_inputs()

    def _L0_attn_setup():
        import jax, jax.numpy as jnp
        import numpy as np
        B, S, D, H = (2, 256, 256, 16)
        DH = D // H
        BW = 128
        K = 4
        _EPS = 1e-06

        def _rmsnorm(x, w):
            return x * jax.lax.rsqrt(jnp.mean(x * x, axis=-1, keepdims=True) + _EPS) * w

        def _l2norm(x):
            return x * jax.lax.rsqrt(jnp.sum(x * x, axis=-1, keepdims=True) + _EPS)

        def _causal_dwconv_silu(x, w):
            k = w.shape[1]
            xp = jnp.pad(x, ((0, 0), (k - 1, 0), (0, 0)))
            mixed = sum((xp[:, i:i + x.shape[1], :] * w[:, i] for i in range(k)))
            return jax.nn.silu(mixed)

        def _forward(hidden, cond_in_W, rot_theta, cond_norm_w, delta_W, qkv_ramp_logit, beta_ramp_logit, ctrl_W, ctrl_b, q_conv_w, k_conv_w, v_conv_w, out_norm_w, out_proj_W, out_proj_b):
            b, s, d = hidden.shape
            h = beta_ramp_logit.shape[0]
            dh = d // h
            p = hidden @ cond_in_W
            bw = p.shape[-1]
            p2 = jnp.moveaxis(p.reshape(b, s, bw // 2, 2), 1, 0)
            c, sn = (jnp.cos(rot_theta), jnp.sin(rot_theta))

            def rot_step(carry, xt):
                s0, s1 = (carry[..., 0], carry[..., 1])
                new = jnp.stack([c * s0 - sn * s1 + xt[..., 0], sn * s0 + c * s1 + xt[..., 1]], axis=-1)
                return (new, new)
            init = jnp.zeros((b, bw // 2, 2), hidden.dtype)
            _, states = jax.lax.scan(rot_step, init, p2)
            cond = _rmsnorm(jnp.moveaxis(states, 0, 1).reshape(b, s, bw), cond_norm_w)
            deltas = cond @ delta_W
            qd, kd, vd, bd = jnp.split(deltas, [d, 2 * d, 3 * d], axis=-1)
            ramp = jax.nn.sigmoid(qkv_ramp_logit)
            qd = qd * ramp[0]
            kd = kd * ramp[1]
            vd = vd * ramp[2]
            bd = bd * jax.nn.sigmoid(beta_ramp_logit)
            ctrl = hidden @ ctrl_W + ctrl_b
            q_l, k_l, v_l, dec_l, bet_l, gate_l = jnp.split(ctrl, [d, 2 * d, 3 * d, 3 * d + h, 3 * d + 2 * h], axis=-1)
            q = _causal_dwconv_silu(q_l + qd, q_conv_w).reshape(b, s, h, dh)
            k = _causal_dwconv_silu(k_l + kd, k_conv_w).reshape(b, s, h, dh)
            v = _causal_dwconv_silu(v_l + vd, v_conv_w).reshape(b, s, h, dh)
            q, k = (_l2norm(q), _l2norm(k))
            beta = jax.nn.sigmoid(bet_l + bd)
            g = jax.nn.sigmoid(dec_l)

            def step(Sst, inp):
                qt, kt, vt, bt, gt = inp
                Sd = gt[..., None, None] * Sst
                kS = jnp.einsum('bhk,bhkv->bhv', kt, Sd)
                Snew = Sd + jnp.einsum('bhk,bhv->bhkv', kt, bt[..., None] * (vt - kS))
                ot = jnp.einsum('bhk,bhkv->bhv', qt, Snew)
                return (Snew, ot)
            xs = tuple((jnp.moveaxis(a, 1, 0) for a in (q, k, v, beta, g)))
            S0 = jnp.zeros((b, h, dh, dh), hidden.dtype)
            _, o = jax.lax.scan(step, S0, xs)
            o = jnp.moveaxis(o, 0, 1)
            gate = gate_l.reshape(b, s, h, dh)
            o = _rmsnorm(o, out_norm_w) * jax.nn.silu(gate)
            return o.reshape(b, s, d) @ out_proj_W.T + out_proj_b
        key = jax.random.key(seed)
        ks = jax.random.split(key, 12)
        n = lambda k, shp, s=0.02: jax.random.normal(k, shp, jnp.float32) * s
        logit001 = float(np.log(0.01 / 0.99))
        ctrl_b = np.zeros(3 * D + 2 * H + D, np.float32)
        ctrl_b[3 * D:3 * D + H] = 1.5
        ctrl_b[3 * D + H:3 * D + 2 * H] = -2.0
        ctrl_b[3 * D + 2 * H:] = -1.5
        conv_base = np.zeros((D, K), np.float32)
        conv_base[:, -1] = 1.0
        return {'hidden': jax.random.normal(ks[0], (B, S, D), jnp.float32), 'cond_in_W': n(ks[1], (D, BW)), 'rot_theta': jax.random.uniform(ks[2], (BW // 2,), jnp.float32, 0.0, 0.5), 'cond_norm_w': jnp.ones((BW,), jnp.float32), 'delta_W': n(ks[3], (BW, 3 * D + H)), 'qkv_ramp_logit': jnp.full((3, D), logit001, jnp.float32), 'beta_ramp_logit': jnp.full((H,), logit001, jnp.float32), 'ctrl_W': n(ks[4], (D, 3 * D + 2 * H + D)), 'ctrl_b': jnp.asarray(ctrl_b), 'q_conv_w': jnp.asarray(conv_base) + n(ks[5], (D, K), 0.05), 'k_conv_w': jnp.asarray(conv_base) + n(ks[6], (D, K), 0.05), 'v_conv_w': jnp.asarray(conv_base) + n(ks[7], (D, K), 0.05), 'out_norm_w': jnp.ones((DH,), jnp.float32), 'out_proj_W': n(ks[8], (D, D)), 'out_proj_b': jnp.zeros((D,), jnp.float32)}
    _L0_attn_all = _L0_attn_setup()
    _L0_attn_in = {k: v for k, v in _L0_attn_all.items() if k in ('cond_in_W', 'rot_theta', 'cond_norm_w', 'delta_W', 'qkv_ramp_logit', 'beta_ramp_logit', 'ctrl_W', 'ctrl_b', 'q_conv_w', 'k_conv_w', 'v_conv_w', 'out_norm_w', 'out_proj_W', 'out_proj_b')}
    del _L0_attn_all

    def _L0_xattn_setup():
        import jax, jax.numpy as jnp
        import numpy as np
        import math
        DIM = 256
        H = 16
        HD = DIM // H // 2
        DEPTH = 4
        LAMBDA_INIT = 0.8 - 0.6 * math.exp(-0.3 * DEPTH)
        SCALE = HD ** (-0.5)
        EPS = 1e-05

        def _sdpa(q, k, v):
            scores = jnp.einsum('bhqd,bhkd->bhqk', q * SCALE, k)
            p = jax.nn.softmax(scores, axis=-1)
            return jnp.einsum('bhqk,bhkd->bhqd', p, v)
        key = jax.random.key(seed)
        ks = jax.random.split(key, 12)
        B, Nq, Nk = (2, 512, 512)
        s = DIM ** (-0.5)
        return {'query': jax.random.normal(ks[0], (B, Nq, DIM), jnp.float32), 'key_': jax.random.normal(ks[1], (B, Nk, DIM), jnp.float32), 'value': jax.random.normal(ks[2], (B, Nk, DIM), jnp.float32), 'Wq': jax.random.normal(ks[3], (DIM, DIM), jnp.float32) * s, 'Wk': jax.random.normal(ks[4], (DIM, DIM), jnp.float32) * s, 'Wv': jax.random.normal(ks[5], (DIM, DIM), jnp.float32) * s, 'Wp': jax.random.normal(ks[6], (DIM, DIM), jnp.float32) * s, 'bp': jnp.zeros((DIM,), jnp.float32), 'lq1': jax.random.normal(ks[7], (HD,), jnp.float32) * 0.1, 'lk1': jax.random.normal(ks[8], (HD,), jnp.float32) * 0.1, 'lq2': jax.random.normal(ks[9], (HD,), jnp.float32) * 0.1, 'lk2': jax.random.normal(ks[10], (HD,), jnp.float32) * 0.1, 'subln_w': jnp.ones((2 * HD,), jnp.float32)}
    _L0_xattn_all = _L0_xattn_setup()
    _L0_xattn_in = {k: v for k, v in _L0_xattn_all.items() if k in ('Wq', 'Wk', 'Wv', 'Wp', 'bp', 'lq1', 'lk1', 'lq2', 'lk2', 'subln_w')}
    del _L0_xattn_all

    def _L0_ffn_setup():
        import jax, jax.numpy as jnp
        import numpy as np
        from jax import lax
        B, L, D = (4, 512, 256)
        E, TOPK = (8, 2)
        K, DIL = (3, 1)
        HID = D // 4
        EPS = 1e-06

        def _rmsnorm(h, w):
            rms = jnp.sqrt(jnp.mean(h * h, axis=-1, keepdims=True) + EPS)
            return w * (h / rms)

        def _forward(x, dw_kernel, dw_bias, pw_w, pw_b, router_w, router_b, expert_w, expert_b, out_w, out_b, norm_w, ff_down_w, ff_down_b, ff_up_w, ff_up_b):
            pad = (K - 1) * DIL
            xc = jnp.transpose(x, (0, 2, 1))
            xc = lax.conv_general_dilated(xc, dw_kernel, window_strides=(1,), padding=((pad, 0),), rhs_dilation=(DIL,), dimension_numbers=('NCH', 'OIH', 'NCH'), feature_group_count=D) + dw_bias[None, :, None]
            xc = jax.nn.silu(jnp.einsum('bdl,ed->bel', xc, pw_w) + pw_b[None, :, None])
            x1 = x + jnp.transpose(xc, (0, 2, 1))
            logits = jnp.einsum('bsd,ed->bse', x1, router_w) + router_b
            top_v, top_i = lax.top_k(logits, TOPK)
            top_w = jax.nn.softmax(top_v, axis=-1)
            rw = jnp.sum(jax.nn.one_hot(top_i, E, dtype=x1.dtype) * top_w[..., None], axis=-2)
            ye = jax.nn.silu(jnp.einsum('bsd,eod->bseo', x1, expert_w) + expert_b)
            combined = jnp.einsum('bse,bseo->bso', rw, ye)
            moe_out = jnp.einsum('bsd,od->bso', combined, out_w) + out_b
            h = _rmsnorm(x1 + moe_out, norm_w)
            ff = jax.nn.gelu(jnp.einsum('bsd,hd->bsh', h, ff_down_w) + ff_down_b, approximate=False)
            ff = jnp.einsum('bsh,dh->bsd', ff, ff_up_w) + ff_up_b
            return h + ff
        key = jax.random.key(seed)
        ks = jax.random.split(key, 16)
        s = 0.02
        return {'x': jax.random.normal(ks[0], (B, L, D), dtype=jnp.float32), 'dw_kernel': jax.random.normal(ks[1], (D, 1, K), dtype=jnp.float32) * s, 'dw_bias': jnp.zeros((D,), dtype=jnp.float32), 'pw_w': jax.random.normal(ks[2], (D, D), dtype=jnp.float32) * s, 'pw_b': jnp.zeros((D,), dtype=jnp.float32), 'router_w': jax.random.normal(ks[3], (E, D), dtype=jnp.float32) * s, 'router_b': jnp.zeros((E,), dtype=jnp.float32), 'expert_w': jax.random.normal(ks[4], (E, D, D), dtype=jnp.float32) * s, 'expert_b': jnp.zeros((E, D), dtype=jnp.float32), 'out_w': jax.random.normal(ks[5], (D, D), dtype=jnp.float32) * s, 'out_b': jnp.zeros((D,), dtype=jnp.float32), 'norm_w': jnp.ones((D,), dtype=jnp.float32), 'ff_down_w': jax.random.normal(ks[6], (HID, D), dtype=jnp.float32) * s, 'ff_down_b': jnp.zeros((HID,), dtype=jnp.float32), 'ff_up_w': jax.random.normal(ks[7], (D, HID), dtype=jnp.float32) * s, 'ff_up_b': jnp.zeros((D,), dtype=jnp.float32)}
    _L0_ffn_all = _L0_ffn_setup()
    _L0_ffn_in = {k: v for k, v in _L0_ffn_all.items() if k in ('dw_kernel', 'dw_bias', 'pw_w', 'pw_b', 'router_w', 'router_b', 'expert_w', 'expert_b', 'out_w', 'out_b', 'norm_w', 'ff_down_w', 'ff_down_b', 'ff_up_w', 'ff_up_b')}
    del _L0_ffn_all
    return {'x': x, 'ctx_1024': ctx_1024, 'L0_attn_cond_in_W': _L0_attn_in['cond_in_W'], 'L0_attn_rot_theta': _L0_attn_in['rot_theta'], 'L0_attn_cond_norm_w': _L0_attn_in['cond_norm_w'], 'L0_attn_delta_W': _L0_attn_in['delta_W'], 'L0_attn_qkv_ramp_logit': _L0_attn_in['qkv_ramp_logit'], 'L0_attn_beta_ramp_logit': _L0_attn_in['beta_ramp_logit'], 'L0_attn_ctrl_W': _L0_attn_in['ctrl_W'], 'L0_attn_ctrl_b': _L0_attn_in['ctrl_b'], 'L0_attn_q_conv_w': _L0_attn_in['q_conv_w'], 'L0_attn_k_conv_w': _L0_attn_in['k_conv_w'], 'L0_attn_v_conv_w': _L0_attn_in['v_conv_w'], 'L0_attn_out_norm_w': _L0_attn_in['out_norm_w'], 'L0_attn_out_proj_W': _L0_attn_in['out_proj_W'], 'L0_attn_out_proj_b': _L0_attn_in['out_proj_b'], 'L0_xattn_Wq': _L0_xattn_in['Wq'], 'L0_xattn_Wk': _L0_xattn_in['Wk'], 'L0_xattn_Wv': _L0_xattn_in['Wv'], 'L0_xattn_Wp': _L0_xattn_in['Wp'], 'L0_xattn_bp': _L0_xattn_in['bp'], 'L0_xattn_lq1': _L0_xattn_in['lq1'], 'L0_xattn_lk1': _L0_xattn_in['lk1'], 'L0_xattn_lq2': _L0_xattn_in['lq2'], 'L0_xattn_lk2': _L0_xattn_in['lk2'], 'L0_xattn_subln_w': _L0_xattn_in['subln_w'], 'L0_ffn_dw_kernel': _L0_ffn_in['dw_kernel'], 'L0_ffn_dw_bias': _L0_ffn_in['dw_bias'], 'L0_ffn_pw_w': _L0_ffn_in['pw_w'], 'L0_ffn_pw_b': _L0_ffn_in['pw_b'], 'L0_ffn_router_w': _L0_ffn_in['router_w'], 'L0_ffn_router_b': _L0_ffn_in['router_b'], 'L0_ffn_expert_w': _L0_ffn_in['expert_w'], 'L0_ffn_expert_b': _L0_ffn_in['expert_b'], 'L0_ffn_out_w': _L0_ffn_in['out_w'], 'L0_ffn_out_b': _L0_ffn_in['out_b'], 'L0_ffn_norm_w': _L0_ffn_in['norm_w'], 'L0_ffn_ff_down_w': _L0_ffn_in['ff_down_w'], 'L0_ffn_ff_down_b': _L0_ffn_in['ff_down_b'], 'L0_ffn_ff_up_w': _L0_ffn_in['ff_up_w'], 'L0_ffn_ff_up_b': _L0_ffn_in['ff_up_b']}

def reference(x, ctx_1024, L0_attn_cond_in_W, L0_attn_rot_theta, L0_attn_cond_norm_w, L0_attn_delta_W, L0_attn_qkv_ramp_logit, L0_attn_beta_ramp_logit, L0_attn_ctrl_W, L0_attn_ctrl_b, L0_attn_q_conv_w, L0_attn_k_conv_w, L0_attn_v_conv_w, L0_attn_out_norm_w, L0_attn_out_proj_W, L0_attn_out_proj_b, L0_xattn_Wq, L0_xattn_Wk, L0_xattn_Wv, L0_xattn_Wp, L0_xattn_bp, L0_xattn_lq1, L0_xattn_lk1, L0_xattn_lq2, L0_xattn_lk2, L0_xattn_subln_w, L0_ffn_dw_kernel, L0_ffn_dw_bias, L0_ffn_pw_w, L0_ffn_pw_b, L0_ffn_router_w, L0_ffn_router_b, L0_ffn_expert_w, L0_ffn_expert_b, L0_ffn_out_w, L0_ffn_out_b, L0_ffn_norm_w, L0_ffn_ff_down_w, L0_ffn_ff_down_b, L0_ffn_ff_up_w, L0_ffn_ff_up_b):
    import jax
    import jax.numpy as jnp

    def _L0_attn_ref(hidden, cond_in_W, rot_theta, cond_norm_w, delta_W, qkv_ramp_logit, beta_ramp_logit, ctrl_W, ctrl_b, q_conv_w, k_conv_w, v_conv_w, out_norm_w, out_proj_W, out_proj_b):
        import jax, jax.numpy as jnp
        import numpy as np
        B, S, D, H = (2, 256, 256, 16)
        DH = D // H
        BW = 128
        K = 4
        _EPS = 1e-06

        def _rmsnorm(x, w):
            return x * jax.lax.rsqrt(jnp.mean(x * x, axis=-1, keepdims=True) + _EPS) * w

        def _l2norm(x):
            return x * jax.lax.rsqrt(jnp.sum(x * x, axis=-1, keepdims=True) + _EPS)

        def _causal_dwconv_silu(x, w):
            k = w.shape[1]
            xp = jnp.pad(x, ((0, 0), (k - 1, 0), (0, 0)))
            mixed = sum((xp[:, i:i + x.shape[1], :] * w[:, i] for i in range(k)))
            return jax.nn.silu(mixed)

        def _forward(hidden, cond_in_W, rot_theta, cond_norm_w, delta_W, qkv_ramp_logit, beta_ramp_logit, ctrl_W, ctrl_b, q_conv_w, k_conv_w, v_conv_w, out_norm_w, out_proj_W, out_proj_b):
            b, s, d = hidden.shape
            h = beta_ramp_logit.shape[0]
            dh = d // h
            p = hidden @ cond_in_W
            bw = p.shape[-1]
            p2 = jnp.moveaxis(p.reshape(b, s, bw // 2, 2), 1, 0)
            c, sn = (jnp.cos(rot_theta), jnp.sin(rot_theta))

            def rot_step(carry, xt):
                s0, s1 = (carry[..., 0], carry[..., 1])
                new = jnp.stack([c * s0 - sn * s1 + xt[..., 0], sn * s0 + c * s1 + xt[..., 1]], axis=-1)
                return (new, new)
            init = jnp.zeros((b, bw // 2, 2), hidden.dtype)
            _, states = jax.lax.scan(rot_step, init, p2)
            cond = _rmsnorm(jnp.moveaxis(states, 0, 1).reshape(b, s, bw), cond_norm_w)
            deltas = cond @ delta_W
            qd, kd, vd, bd = jnp.split(deltas, [d, 2 * d, 3 * d], axis=-1)
            ramp = jax.nn.sigmoid(qkv_ramp_logit)
            qd = qd * ramp[0]
            kd = kd * ramp[1]
            vd = vd * ramp[2]
            bd = bd * jax.nn.sigmoid(beta_ramp_logit)
            ctrl = hidden @ ctrl_W + ctrl_b
            q_l, k_l, v_l, dec_l, bet_l, gate_l = jnp.split(ctrl, [d, 2 * d, 3 * d, 3 * d + h, 3 * d + 2 * h], axis=-1)
            q = _causal_dwconv_silu(q_l + qd, q_conv_w).reshape(b, s, h, dh)
            k = _causal_dwconv_silu(k_l + kd, k_conv_w).reshape(b, s, h, dh)
            v = _causal_dwconv_silu(v_l + vd, v_conv_w).reshape(b, s, h, dh)
            q, k = (_l2norm(q), _l2norm(k))
            beta = jax.nn.sigmoid(bet_l + bd)
            g = jax.nn.sigmoid(dec_l)

            def step(Sst, inp):
                qt, kt, vt, bt, gt = inp
                Sd = gt[..., None, None] * Sst
                kS = jnp.einsum('bhk,bhkv->bhv', kt, Sd)
                Snew = Sd + jnp.einsum('bhk,bhv->bhkv', kt, bt[..., None] * (vt - kS))
                ot = jnp.einsum('bhk,bhkv->bhv', qt, Snew)
                return (Snew, ot)
            xs = tuple((jnp.moveaxis(a, 1, 0) for a in (q, k, v, beta, g)))
            S0 = jnp.zeros((b, h, dh, dh), hidden.dtype)
            _, o = jax.lax.scan(step, S0, xs)
            o = jnp.moveaxis(o, 0, 1)
            gate = gate_l.reshape(b, s, h, dh)
            o = _rmsnorm(o, out_norm_w) * jax.nn.silu(gate)
            return o.reshape(b, s, d) @ out_proj_W.T + out_proj_b
        return _forward(hidden, cond_in_W, rot_theta, cond_norm_w, delta_W, qkv_ramp_logit, beta_ramp_logit, ctrl_W, ctrl_b, q_conv_w, k_conv_w, v_conv_w, out_norm_w, out_proj_W, out_proj_b)

    def _L0_xattn_ref(query, key_, value, Wq, Wk, Wv, Wp, bp, lq1, lk1, lq2, lk2, subln_w):
        import jax, jax.numpy as jnp
        import numpy as np
        import math
        DIM = 256
        H = 16
        HD = DIM // H // 2
        DEPTH = 4
        LAMBDA_INIT = 0.8 - 0.6 * math.exp(-0.3 * DEPTH)
        SCALE = HD ** (-0.5)
        EPS = 1e-05

        def _sdpa(q, k, v):
            scores = jnp.einsum('bhqd,bhkd->bhqk', q * SCALE, k)
            p = jax.nn.softmax(scores, axis=-1)
            return jnp.einsum('bhqk,bhkd->bhqd', p, v)
        B, Nq, C = query.shape
        Nk = key_.shape[1]
        q = (query @ Wq.T).reshape(B, Nq, 2 * H, HD).transpose(0, 2, 1, 3)
        k = (key_ @ Wk.T).reshape(B, Nk, 2 * H, HD).transpose(0, 2, 1, 3)
        v = (value @ Wv.T).reshape(B, Nk, H, 2 * HD).transpose(0, 2, 1, 3)
        q1, q2 = (q[:, :H], q[:, H:])
        k1, k2 = (k[:, :H], k[:, H:])
        a1 = _sdpa(q1, k1, v)
        a2 = _sdpa(q2, k2, v)
        lam1 = jnp.exp(jnp.sum(lq1 * lk1))
        lam2 = jnp.exp(jnp.sum(lq2 * lk2))
        lam = lam1 - lam2 + LAMBDA_INIT
        attn = a1 - lam * a2
        attn = attn.transpose(0, 2, 1, 3)
        attn = attn * jax.lax.rsqrt(jnp.mean(attn * attn, axis=-1, keepdims=True) + EPS)
        attn = attn * subln_w
        attn = attn * (1.0 - LAMBDA_INIT)
        attn = attn.reshape(B, Nq, C)
        return attn @ Wp.T + bp

    def _L0_ffn_ref(x, dw_kernel, dw_bias, pw_w, pw_b, router_w, router_b, expert_w, expert_b, out_w, out_b, norm_w, ff_down_w, ff_down_b, ff_up_w, ff_up_b):
        import jax, jax.numpy as jnp
        import numpy as np
        from jax import lax
        B, L, D = (4, 512, 256)
        E, TOPK = (8, 2)
        K, DIL = (3, 1)
        HID = D // 4
        EPS = 1e-06

        def _rmsnorm(h, w):
            rms = jnp.sqrt(jnp.mean(h * h, axis=-1, keepdims=True) + EPS)
            return w * (h / rms)

        def _forward(x, dw_kernel, dw_bias, pw_w, pw_b, router_w, router_b, expert_w, expert_b, out_w, out_b, norm_w, ff_down_w, ff_down_b, ff_up_w, ff_up_b):
            pad = (K - 1) * DIL
            xc = jnp.transpose(x, (0, 2, 1))
            xc = lax.conv_general_dilated(xc, dw_kernel, window_strides=(1,), padding=((pad, 0),), rhs_dilation=(DIL,), dimension_numbers=('NCH', 'OIH', 'NCH'), feature_group_count=D) + dw_bias[None, :, None]
            xc = jax.nn.silu(jnp.einsum('bdl,ed->bel', xc, pw_w) + pw_b[None, :, None])
            x1 = x + jnp.transpose(xc, (0, 2, 1))
            logits = jnp.einsum('bsd,ed->bse', x1, router_w) + router_b
            top_v, top_i = lax.top_k(logits, TOPK)
            top_w = jax.nn.softmax(top_v, axis=-1)
            rw = jnp.sum(jax.nn.one_hot(top_i, E, dtype=x1.dtype) * top_w[..., None], axis=-2)
            ye = jax.nn.silu(jnp.einsum('bsd,eod->bseo', x1, expert_w) + expert_b)
            combined = jnp.einsum('bse,bseo->bso', rw, ye)
            moe_out = jnp.einsum('bsd,od->bso', combined, out_w) + out_b
            h = _rmsnorm(x1 + moe_out, norm_w)
            ff = jax.nn.gelu(jnp.einsum('bsd,hd->bsh', h, ff_down_w) + ff_down_b, approximate=False)
            ff = jnp.einsum('bsh,dh->bsd', ff, ff_up_w) + ff_up_b
            return h + ff
        return _forward(x, dw_kernel, dw_bias, pw_w, pw_b, router_w, router_b, expert_w, expert_b, out_w, out_b, norm_w, ff_down_w, ff_down_b, ff_up_w, ff_up_b)
    x = x + _L0_attn_ref(_layernorm(x, axis=-1), L0_attn_cond_in_W, L0_attn_rot_theta, L0_attn_cond_norm_w, L0_attn_delta_W, L0_attn_qkv_ramp_logit, L0_attn_beta_ramp_logit, L0_attn_ctrl_W, L0_attn_ctrl_b, L0_attn_q_conv_w, L0_attn_k_conv_w, L0_attn_v_conv_w, L0_attn_out_norm_w, L0_attn_out_proj_W, L0_attn_out_proj_b)
    x = x + _L0_xattn_ref(_layernorm(x, axis=-1), ctx_1024, ctx_1024, L0_xattn_Wq, L0_xattn_Wk, L0_xattn_Wv, L0_xattn_Wp, L0_xattn_bp, L0_xattn_lq1, L0_xattn_lk1, L0_xattn_lq2, L0_xattn_lk2, L0_xattn_subln_w)
    x = x + _L0_ffn_ref(_layernorm(x, axis=-1), L0_ffn_dw_kernel, L0_ffn_dw_bias, L0_ffn_pw_w, L0_ffn_pw_b, L0_ffn_router_w, L0_ffn_router_b, L0_ffn_expert_w, L0_ffn_expert_b, L0_ffn_out_w, L0_ffn_out_b, L0_ffn_norm_w, L0_ffn_ff_down_w, L0_ffn_ff_down_b, L0_ffn_ff_up_w, L0_ffn_ff_up_b)
    return x

_drawn_inputs = setup_inputs


def setup_inputs(seed=0):
    import zlib

    import numpy as np

    out = dict(_drawn_inputs(seed))
    spreads = {'L0_attn_cond_norm_w': (1.0, 0.6),
     'L0_attn_qkv_ramp_logit': (-4.595119953155518, 0.6),
     'L0_attn_beta_ramp_logit': (-4.595119953155518, 0.6),
     'L0_attn_out_norm_w': (1.0, 0.6),
     'L0_attn_out_proj_b': (0.0, 0.1),
     'L0_xattn_bp': (0.0, 0.1),
     'L0_xattn_subln_w': (1.0, 0.2),
     'L0_ffn_dw_bias': (0.0, 0.8),
     'L0_ffn_pw_b': (0.0, 0.297),
     'L0_ffn_router_b': (0.0, 0.8),
     'L0_ffn_expert_b': (0.0, 0.8),
     'L0_ffn_out_b': (0.0, 0.1),
     'L0_ffn_norm_w': (1.0, 0.2),
     'L0_ffn_ff_down_b': (0.0, 0.8),
     'L0_ffn_ff_up_b': (0.0, 0.1)}
    factors = {'L0_attn_cond_in_W': 8.0,
     'L0_attn_rot_theta': 8.0,
     'L0_attn_delta_W': 8.0,
     'L0_xattn_lq2': 5.367,
     'L0_xattn_lk2': 23.634,
     'L0_ffn_dw_kernel': 8.0,
     'L0_ffn_pw_w': 7.26,
     'L0_ffn_router_w': 3.626,
     'L0_ffn_expert_w': 3.099,
     'L0_ffn_out_w': 2.913,
     'L0_ffn_ff_down_w': 4.243,
     'L0_ffn_ff_up_w': 3.978,
     'L0_xattn_lq1': 3.933,
     'L0_xattn_lk1': 3.615}
    for name, (base, spread) in spreads.items():
        noise = np.random.default_rng([zlib.crc32(name.encode()), seed]).standard_normal(out[name].shape)
        drawn = base * np.exp(spread * noise) if base else spread * noise
        out[name] = jnp.asarray(drawn.astype(out[name].dtype))
    for name, factor in factors.items():
        out[name] = (out[name] * factor).astype(out[name].dtype)
    return out
```

```python
from contextlib import ExitStack

import concourse.bass as bass
from concourse import mybir

F32 = mybir.dt.float32
BF16 = mybir.dt.bfloat16
U32 = mybir.dt.uint32
ACT = mybir.ActivationFunctionType
ALU = mybir.AluOpType
AX = mybir.AxisListType

P = 128
B, S, D = 4, 1024, 256
H, DH = 16, 16
NK = 64
NE, HID = 8, 64
KC = D // P
TB = P
T = B * TB
NI = S // TB
CH = 16
NC = TB // CH
G = 2
HG = H // G
NP_ = B * G * NC
NSUB = NC * G
LAMBDA_INIT = 0.8 - 0.6 * 2.718281828459045 ** (-0.3 * 4)
XSCALE = 8 ** -0.5

WEIGHTS = [("cin", KC * 256), ("dw", 1056), ("ctrl", KC * 1312), ("wo", KC * D), ("wq", KC * D), ("wp", KC * D),
           ("pw", KC * D), ("rw", KC * NE), ("ew", KC * NE * D), ("ow", KC * D), ("normw", D),
           ("ffd", KC * HID), ("ffu", D)]
CONSTS = [("ident", P), ("swap", P), ("ones", P), ("bones", P), ("tri", P), ("negones", P), ("delta", P),
          ("triblk", P), ("bd", HG), ("mc", NC), ("neg", CH), ("hh", 16), ("half", 2), ("iota", NE), ("sgn", 1), ("dup", 2)]
COLUMNS = [("bproj", 10), ("conv", 24), ("theta", 1), ("condnorm", 1), ("outnorm", 1), ("subln", 1),
           ("pwb", 2), ("dwk", 6), ("dwb", 2), ("fdb", 1), ("lam", 32)]
SCRATCH = [("ramp", 1056), ("wk", KC * D), ("wv", KC * D), ("ctx", KC * B * NK), ("ctxd", KC * B * 2 * NK)]
BIASES = [("e", NE * D), ("out", D), ("wo", D), ("xp", D), ("up", D), ("router", NE), ("db", 32)]


def offsets(parts):
    at, out = 0, {}
    for name, size in parts:
        out[name] = (at, at + size)
        at += size
    return out, at


WOFF, NW = offsets(WEIGHTS)
COFF, NCON = offsets(CONSTS)
LOFF, NCOL = offsets(COLUMNS)
SOFF, NSCR = offsets(SCRATCH)
BOFF, NBIAS = offsets(BIASES)


class Event:

    def __init__(self, sem, per=1):
        self.sem, self.per = sem, per

    def at(self, i, k=1):
        return i * self.per + k


class Chain:

    def __init__(self, eng, sem, i=0, per=0):
        self.eng, self.sem, self.i, self.per, self.count = eng, sem, i, per, 0

    def link(self, ins):
        self.count += 1
        ins.then_inc(self.sem, 1)

    def wait(self):
        self.eng.wait_ge(self.sem, self.i * self.per + self.count if self.per else self.count)


DVE_LINKS = 172
ACT_LINKS = 12


def build(nc, x, out, weights, consts, cols, scratch, biases, teye, dbg=None):
    ctx = ExitStack()
    with ctx:
        def sb(name, shape, dt=F32):
            return ctx.enter_context(nc.sbuf_tensor(name, shape, dt))

        def sem(name):
            return ctx.enter_context(nc.semaphore(name))

        def event(name, per=1):
            return Event(sem(name), per)

        bank = [ctx.enter_context(nc.psum_tensor(f"bank{n}", [P, 512], F32)) for n in range(8)]

        w_sb = sb("w_sb", [P, NW])
        c_sb = sb("c_sb", [P, NCON])
        l_sb = sb("l_sb", [P, NCOL])

        def W(name):
            return w_sb[:, WOFF[name][0]:WOFF[name][1]]

        def C(name):
            return c_sb[:, COFF[name][0]:COFF[name][1]]

        def L(name, a=0, b=None):
            lo, hi = LOFF[name]
            return l_sb[:, lo + a:(hi if b is None else lo + b)]

        cin = W("cin").rearrange("p (k n) -> p k n", k=KC)
        ctrl = W("ctrl").rearrange("p (k n) -> p k n", k=KC)
        wo = W("wo").rearrange("p (k n) -> p k n", k=KC)
        wq = W("wq").rearrange("p (k n) -> p k n", k=KC)
        wp = W("wp").rearrange("p (k n) -> p k n", k=KC)
        pw = W("pw").rearrange("p (k n) -> p k n", k=KC)
        rw_w = W("rw").rearrange("p (k n) -> p k n", k=KC)
        ew = W("ew").rearrange("p (k n) -> p k n", k=KC)
        ow = W("ow").rearrange("p (k n) -> p k n", k=KC)
        ffd = W("ffd").rearrange("p (k n) -> p k n", k=KC)
        ffu = W("ffu")[0:HID, :]
        dw = W("dw")
        ident = C("ident")
        bd = C("bd")
        cosT = sb("cosT", [P, TB])
        sinT = sb("sinT", [P, TB])
        small = sb("small", [P, 64])
        bias3 = sb("bias3", [3, NBIAS], BF16)
        ones3 = sb("ones3", [3, P], BF16)
        kbx = sb("kbx", [P, 2, B, 16 * NK])
        vx = sb("vx", [P, B, H, 34])
        nlam = small[:, 0:1]
        eps5 = small[:, 1:2]
        eps6 = small[:, 2:3]
        spare = small[:, 60:61]

        zc = sb("zc", [P, B])
        state = sb("state", [P, B, G, DH])

        xt = sb("xt", [P, B, D])
        hid = sb("hid", [P, B, D])
        hT = sb("hT", [P, KC, T])
        pre = sb("pre", [P, 6, B, TB + 3])
        qkv = sb("qkv", [P, 6, T])
        rota = sb("rota", [P, T])
        rotb = sb("rotb", [P, T])
        kn = sb("kn", [P, G, T])
        kq = sb("kq", [P, G, B, NC, 2, CH])
        sg = sb("sg", [P, G, T])
        stat = sb("stat", [P, B, 6])
        mv = sb("mv", [P, B, 2])
        rstd = sb("rstd", [P, B])
        edb = sb("edb", [P, B, 32])
        lgc = sb("lgc", [P, B, H])
        btc = sb("btc", [P, B, H])
        pk = sb("pk", [P, 8, NP_])
        Gp, GCp, Bp, eG, eGC, eD, bG, ors = [pk[:, n, :] for n in range(8)]
        M1 = sb("M1", [P, NP_, CH])
        M2 = sb("M2", [P, NP_, CH])
        M3 = sb("M3", [P, NP_, CH])
        M4 = sb("M4", [P, NP_, CH])
        M5 = sb("M5", [P, NP_, CH])
        Tm = sb("Tm", [P, 4, CH, CH])
        M2b = sb("M2b", [P, 2 * NP_, CH])
        obuf = M1[:, :, :].rearrange("p (g n) v -> p g n v", g=G)
        vsel3 = hid[:, :, :].rearrange("p b (n v) -> p (b n) v", v=DH)
        vsel = vsel3.rearrange("p (g b c) v -> p g b c v", g=G, b=B)
        kbd = sb("kbd", [P, 2, B, P])
        qbd = sb("qbd", [P, 2, B, P])
        tbd, mbd, ktb = [qkv[:, 2 * n:2 * n + 2, :].rearrange("p r (b m) -> p r b m", b=B) for n in range(3)]
        usm = sb("usm", [P, 2, 4, B * DH])

        fT = sb("fT", [P, KC, B, TB + 2])
        rwt = sb("rwt", [P, 8, B, NE])
        idx = sb("idx", [P, B, 8], U32)

        beta = hid[:, :, :].rearrange("p b d -> p (b d)").rearrange("p (g t) -> p g t", g=G)
        crs = sg[:, 0, :]
        x1 = xt
        n2 = hid
        n2T = hT
        qx = qkv[:, 0:2, :]
        prob = qkv[:, 2:4, :].rearrange("p k t -> p (k t)").rearrange("p (h f n) -> p h f n", h=8, f=2)
        probT = qkv[:, 4:6, :].rearrange("p k t -> p (k t)").rearrange("p (h t) -> p h t", h=8)
        ax = kq[:, :, :, :, :, :].rearrange("p g b c x t -> p (g b c x t)")[:, 0:1024].rearrange("p (b h v) -> p b h v", b=B, h=H)
        at2 = kq[:, :, :, :, :, :].rearrange("p g b c x t -> p (g b c x t)")[:, 1024:2048]
        dcv = kn
        x1T = hT
        comb = M3[:, :, :].rearrange("p n t -> p (n t)").rearrange("p (b d) -> p b d", b=B)
        combT = M4[:, :, :].rearrange("p n t -> p (n t)").rearrange("p (k t) -> p k t", k=KC)
        ye = M2b[:, :, :].rearrange("p n t -> p (n t)").rearrange("p (r n) -> p r n", r=4)
        hx = M1[:, :, :].rearrange("p n t -> p (n t)").rearrange("p (b d) -> p b d", b=B)
        hTT = M2[:, :, :].rearrange("p n t -> p (n t)").rearrange("p (k t) -> p k t", k=KC)
        gT = rota[0:HID, :]
        ot = M5[:, :, :].rearrange("p n t -> p (n t)").rearrange("p (b d) -> p b d", b=B)
        sT = sg

        def flat(t3):
            return t3.rearrange("p a b -> p (a b)")

        bias_row = kbx[0:1, 0, :, :].rearrange("p b n -> p (b n)")[:, 0:NBIAS]
        bias_rest = kbx[0:1, 1, :, :].rearrange("p b n -> p (b n)")[:, 0:NBIAS]
        bias_part = [M2b[0:1, :, :].rearrange("p n t -> p (n t)")[:, 0:NBIAS // 2].bitcast(BF16),
                     pre[0:1, :, :, :].rearrange("p j b t -> p (j b t)")[:, 0:NBIAS // 2].bitcast(BF16),
                     kq[0:1, :, :, :, :, :].rearrange("p g b c x t -> p (g b c x t)")[:, 0:NBIAS // 2].bitcast(BF16)]
        vb = M5[:, :, :].rearrange("p (g b c) v -> p g b c v", g=G, b=B)
        dbg_srcs = []

        ld_w, ld_c, ld_b3, st_dbg = sem("ld_w"), sem("ld_c"), sem("ld_b3"), sem("st_dbg")
        vset, aset = sem("vset"), sem("aset")
        su = {n: sem("su_" + n) for n in ("trig_in", "trig", "split", "kproj", "vproj", "kv_sb", "exp_in", "exp_out", "ready", "tables")}
        x_in, x_out = event("x_in", 16), event("x_out", 16)
        dchain, achain = sem("dchain"), sem("achain")
        ev = {}
        for name, per in [("var", 3), ("rstd", 3), ("normed", 4), ("tr_ps", 6), ("tr_a", 6), ("tr_v", 6),
                          ("rot_ps", 1), ("y", 1), ("y2_ps", 1), ("z", 1), ("zsq", 1), ("zsum_ps", 1), ("crs", 1), ("cond", 1),
                          ("proj_ps", 10), ("pre_sb", 10), ("conv", 6), ("act_silu", 6), ("sq", 4), ("sum_ps", 4), ("rs", 4), ("qk_norm", 4),
                          ("db_ps", 1), ("db_sb", 1), ("db_exp", 1), ("db_one", 1), ("lg", 1), ("bt", 1), ("xpand", 2), ("lrep", 1), ("gsum_ps", 1), ("gsel", 1), ("gexp", 1),
                          ("grow_ps", 1), ("d_ready", 1), ("e_ready", 1), ("kbd", 32), ("qbd", 16), ("raw_ps", 16), ("am", 4), ("tinv", 1),
                          ("tmbd", 16), ("ks_ps", 16), ("r_ready", 16), ("kt_ps", 16), ("kt_sb", 16), ("u_ps", 16), ("u_sb", 16), ("ds_ps", 16), ("s_new", 16),
                          ("osq", 1), ("osum", 1), ("ors", 1), ("og", 1), ("wo_ps", 1), ("qx_ps", 1), ("qx_sb", 1), ("sc_ps", 8), ("psub", 8), ("pexp", 8),
                          ("pt_ps", 8), ("pt_a", 8), ("pt_v", 8), ("pv_ps", 8), ("a_sb", 8), ("asq", 1), ("asum", 1), ("ars", 1), ("wp_ps", 1),
                          ("dconv", 1), ("pw_ps", 1), ("pws", 1), ("x1T", 1), ("lgt_ps", 1), ("top", 1), ("texp", 1), ("moe_ps", 16), ("moe_act", 16), ("moe_acc", 16),
                          ("mo_ps", 1), ("mo_sb", 1), ("hrs", 1), ("hn", 1), ("ffd_ps", 1), ("gelu", 1), ("xh", 1), ("ffu_ps", 1), ("done", 1)]:
            ev[name] = event(name, per)

        block = ctx.enter_context(nc.Block())

        @block.sync
        def _(sp):
            sp.dma_start(l_sb[:, :], cols[:, :]).then_inc(ld_c, 16)
            sp.dma_start(c_sb[:, :], consts[:, :]).then_inc(ld_c, 16)
            sp.dma_start(bias_row, biases[:, :]).then_inc(ld_c, 16)
            sp.dma_start(Tm[:, :, :, :].rearrange("p a b c -> p (a b c)"), teye[:, :]).then_inc(ld_c, 16)
            for (name, dst) in (("ramp", flat(qkv[:, 0:3, :])[:, 0:1056]), ("wk", flat(hT[:, 0:1, :])), ("wv", flat(hT[:, 1:2, :])),
                                ("ctx", flat(kn[:, 0:1, :])), ("ctxd", flat(xt[:, :, :]))):
                sp.dma_start(dst, scratch[:, SOFF[name][0]:SOFF[name][1]]).then_inc(ld_w, 16)
            sp.dma_start(w_sb[:, :], weights[:, :]).then_inc(ld_w, 16)
            sp.wait_ge(su["split"], 1)
            for n in range(3):
                sp.dma_start(bias3[n:n + 1, :], bias_part[n]).then_inc(ld_b3, 16)
            sp.wait_ge(su["ready"], 1)
            sp.dma_start(xt[:, :, :], x[:, 0:TB, :].rearrange("b p d -> p b d")).then_inc(x_in.sem, 16)
            with sp.Fori(1, NI) as i:
                sp.wait_ge(ev["done"].sem, i)
                sp.dma_start(out[:, bass.ds((i - 1) * TB, TB), :].rearrange("b p d -> p b d"), ot).then_inc(x_out.sem, 16)
                sp.wait_ge(x_out.sem, i * 16)
                sp.dma_start(xt[:, :, :], x[:, bass.ds(i * TB, TB), :].rearrange("b p d -> p b d")).then_inc(x_in.sem, 16)
            sp.wait_ge(ev["done"].sem, NI)
            sp.dma_start(out[:, S - TB:S, :].rearrange("b p d -> p b d"), ot).then_inc(x_out.sem, 16)
            sp.wait_ge(x_out.sem, 16 * NI)
            if dbg is not None:
                for n, src in enumerate(dbg_srcs):
                    sp.dma_start(dbg[n, :, 0:src.shape[1]], src).then_inc(st_dbg, 16)
                sp.wait_ge(st_dbg, 16 * len(dbg_srcs))

        @block.gpsimd
        def _(pool):
            with pool.Fori(0, NI) as i:
                def up(name, k=1):
                    pool.wait_ge(ev[name].sem, ev[name].at(i, k))

                def mask4(out_, in_, m):
                    return nc.gpsimd.tensor_tensor(out_, in_, m, ALU.mult)

                up("lg")
                up("bt")
                for n, (src, dst) in enumerate(((lgc, rota), (btc, rotb))):
                    mask4(dst[:, :].rearrange("p (a c h) -> p a c h", a=B * G, c=NC),
                          src[:, :, :].rearrange("p b (g h) -> p (b g) h", g=G).unsqueeze(2).to_broadcast([P, B * G, NC, HG]),
                          C("mc").unsqueeze(1).unsqueeze(3).to_broadcast([P, B * G, NC, HG])).then_inc(ev["xpand"].sem, 1)
                nc.gpsimd.tensor_copy(M1[:, :, :], flat(lgc[:, :, :]).unsqueeze(2).to_broadcast([P, B * H, CH])).then_inc(ev["lrep"].sem, 1)

                def bdiag(dst, src, g, c, name):
                    mask4(dst.rearrange("p b (h t) -> p b h t", h=HG),
                          src.rearrange("p (b c t) -> p b c t", b=B, c=NC)[:, :, c, :].unsqueeze(2).to_broadcast([P, B, HG, CH]),
                          bd.unsqueeze(1).unsqueeze(3).to_broadcast([P, B, HG, CH])).then_inc(ev[name].sem, 1)

                up("qk_norm", 4)
                for s in range(NSUB):
                    if s >= 2:
                        up("raw_ps", s - 1)
                    bdiag(kbd[:, s % 2, :, :], kn[:, s // NC, :], s // NC, s % NC, "kbd")
                for s in range(NSUB):
                    c, g = s // G, s % G
                    if s < 2:
                        up("raw_ps", 15 + s)
                    else:
                        up("kt_ps", s - 1)
                        up("ks_ps", s - 1)
                    bdiag(kbd[:, s % 2, :, :], kn[:, g, :], g, c, "kbd")
                    mask4(qbd[:, s % 2, :, :].rearrange("p b (h t) -> p b h t", h=HG),
                          kq[:, g, :, c, 1, :].unsqueeze(2).to_broadcast([P, B, HG, CH]),
                          bd.unsqueeze(1).unsqueeze(3).to_broadcast([P, B, HG, CH])).then_inc(ev["qbd"].sem, 1)
                up("s_new", NSUB)
                o2 = M1[:, :, :].rearrange("p n v -> p (n v)")
                nc.gpsimd.tensor_tensor(M2[:, :, :].rearrange("p n t -> p (n t)"), o2, o2, ALU.mult).then_inc(ev["osq"].sem, 1)
                up("a_sb", 8)
                a2 = ax.rearrange("p b h v -> p (b h v)")
                nc.gpsimd.tensor_tensor(at2, a2, a2, ALU.mult).then_inc(ev["asq"].sem, 1)
                up("hn")
                nc.gpsimd.tensor_tensor(flat(xt[:, :, :]), flat(xt[:, :, :]), flat(hx), ALU.add).then_inc(ev["xh"].sem, 1)

        @block.scalar
        def _(act):
            ch = Chain(act, aset)
            act.wait_ge(su["trig_in"], 1)
            nc.scalar.activation(small[:, 16:18], small[:, 18:20], ACT.Sin).then_inc(su["trig"], 1)
            act.wait_ge(su["exp_in"], 1)
            act.wait_ge(ld_w, 16 * 6)
            nc.scalar.activation(flat(qkv[:, 0:3, :])[:, 0:1056], flat(qkv[:, 0:3, :])[:, 0:1056], ACT.Exp, scale=-1.0)
            nc.scalar.activation(small[:, 20:22], small[:, 22:24], ACT.Exp).then_inc(su["exp_out"], 1)
            act.wait_ge(su["kproj"], 1)
            for h2 in range(2):
                nc.scalar.copy(kn[:, 1, h2 * 256:h2 * 256 + 256], bank[h2][:, 0:256])
            act.wait_ge(su["vproj"], 1)
            for n in range(2):
                nc.scalar.copy(M3[:, 32 * n:32 * n + 32, :].rearrange("p n t -> p (n t)"), bank[2 + n][:, :]).then_inc(su["kv_sb"], 1)

            with act.Fori(0, NI) as i:
                ch = Chain(act, achain, i, ACT_LINKS)

                def up(name, k=1):
                    act.wait_ge(ev[name].sem, ev[name].at(i, k))

                def fin(name, ins):
                    ins.then_inc(ev[name].sem, 1)

                def inv_sqrt(dst, src, tmp, eps, scale, name):
                    ch.link(nc.scalar.activation(tmp, src, ACT.Ln, bias=eps, scale=scale))
                    ch.wait()
                    fin(name, nc.scalar.activation(dst, tmp, ACT.Exp, scale=-0.5))

                def layer_rstd(k):
                    up("var", k)
                    ch.link(nc.scalar.activation(rstd[:, :], mv[:, :, 1], ACT.Ln, bias=eps5))
                    ch.wait()
                    fin("rstd", nc.scalar.activation(rstd[:, :], rstd[:, :], ACT.Exp, scale=-0.5))

                layer_rstd(1)
                up("tr_ps", 1)
                fin("tr_a", nc.scalar.copy(hT[:, 0, :], bank[0][:, :]))
                up("z")
                fin("zsq", nc.scalar.activation(qkv[:, 1, :], qkv[:, 0, :], ACT.Square))
                up("zsum_ps")
                inv_sqrt(crs, bank[5][:, :], crs, eps6, 1.0 / P, "crs")
                for j in range(10):
                    up("proj_ps", j + 1)
                    src = bank[j % 4][:, :]
                    if j < 2:
                        fin("pre_sb", nc.scalar.activation(beta[:, j, :], src, ACT.Exp, bias=small[:, 40 + j:41 + j], scale=-1.0))
                    elif j < 8:
                        fin("pre_sb", nc.scalar.activation(pre[:, j - 2, :, 3:TB + 3], src.rearrange("p (b t) -> p b t", b=B),
                                                           ACT.Identity, bias=L("bproj", j - 2, j - 1)))
                    else:
                        fin("pre_sb", nc.scalar.activation(sg[:, j - 8, :], src, ACT.Silu, bias=L("bproj", j - 2, j - 1)))
                for j in range(6):
                    up("conv", j + 1)
                    fin("act_silu", nc.scalar.activation(qkv[:, j, :], qkv[:, j, :], ACT.Silu))
                up("act_silu", 6)
                up("db_ps")
                for j in range(4):
                    if j >= 2:
                        up("sum_ps", j - 1)
                    fin("sq", nc.scalar.activation((rota, rotb)[j % 2][:, :], qkv[:, j, :], ACT.Square))
                for j in range(4):
                    up("sum_ps", j + 1)
                    if j >= 2:
                        up("qk_norm", j - 1)
                    tmp = (M2, M4)[j % 2][:, :, :].rearrange("p n t -> p (n t)")[:, 0:512]
                    inv_sqrt(tmp, bank[4 + j % 2][:, :], tmp, eps6, 1.0, "rs")
                up("db_sb")
                up("qk_norm", 4)
                fin("db_exp", nc.scalar.activation(edb[:, :, :], edb[:, :, :], ACT.Exp, scale=-1.0))
                up("db_one")
                fin("lg", nc.scalar.activation(lgc[:, :, :], edb[:, :, 0:H], ACT.Ln))
                up("gsel")
                nc.scalar.activation(eG, Gp, ACT.Exp)
                nc.scalar.activation(eGC, GCp, ACT.Exp)
                fin("gexp", nc.scalar.activation(eD, eD, ACT.Exp))
                up("d_ready")
                fin("e_ready", nc.scalar.activation(flat(M2[:, :, :]), flat(M2[:, :, :]), ACT.Exp))
                for s in range(NSUB):
                    up("kt_ps", s + 1)
                    if s >= 2:
                        up("ds_ps", s - 1)
                    fin("kt_sb", nc.scalar.copy(flat(ktb[:, s % 2, :, :]), bank[6][:, :]))
                up("osum")
                inv_sqrt(ors, ors, ors, eps6, 1.0 / DH, "ors")

                layer_rstd(2)
                up("tr_ps", 2)
                fin("tr_a", nc.scalar.copy(n2T[:, 0, :], bank[0][:, :]))
                up("qx_ps")
                nc.scalar.copy(qx[:, 0, :], bank[2][:, :])
                fin("qx_sb", nc.scalar.copy(qx[:, 1, :], bank[3][:, :]))
                for u in range(8):
                    up("psub", u + 1)
                    fin("pexp", nc.scalar.activation(prob.rearrange("p h f n -> p (h f n)"), prob.rearrange("p h f n -> p (h f n)"), ACT.Exp, scale=XSCALE))
                    up("pt_ps", u + 1)
                    if u:
                        up("pv_ps", u)
                    fin("pt_a", nc.scalar.copy(probT[:, 0:4, :].rearrange("p h t -> p (h t)"), bank[2][:, :]))
                up("asum")
                inv_sqrt(ors, ors, ors, eps5, 1.0 / DH, "ars")
                up("tr_ps", 3)
                fin("tr_a", nc.scalar.copy(n2T[:, 0, :], bank[0][:, :]))

                layer_rstd(3)
                up("tr_ps", 4)
                fin("tr_a", nc.scalar.copy(fT[:, 0, :, 2:TB + 2], bank[0][:, :].rearrange("p (b t) -> p b t", b=B)))
                up("pw_ps")
                nc.scalar.activation(sT[:, 0, :], bank[2][:, :], ACT.Silu, bias=L("pwb", 0, 1))
                fin("pws", nc.scalar.activation(sT[:, 1, :], bank[3][:, :], ACT.Silu, bias=L("pwb", 1, 2)))
                up("top")
                fin("texp", nc.scalar.activation(rwt[:, 3, :, 1], rwt[:, 3, :, 0], ACT.Exp))
                for u in range(16):
                    up("moe_ps", u + 1)
                    if u >= 4:
                        up("moe_acc", u - 3)
                    fin("moe_act", nc.scalar.activation(ye[:, u % 4, :], bank[4 + u % 4][:, :], ACT.Silu))
                up("tr_ps", 5)
                fin("tr_a", nc.scalar.copy(combT[:, 0, :], bank[0][:, :]))
                up("mo_sb")
                for b in range(B):
                    last = nc.scalar.activation(ye[:, b // 2, (b % 2) * D:(b % 2) * D + D], hx[:, b, :], ACT.Square, accum_out=rstd[:, b:b + 1])
                ch.link(last)
                ch.wait()
                inv_sqrt(rstd[:, :], rstd[:, :], rstd[:, :], eps6, 1.0 / D, "hrs")
                up("tr_ps", 6)
                fin("tr_a", nc.scalar.copy(hTT[:, 0, :], bank[0][:, :]))
                up("ffd_ps")
                fin("gelu", nc.scalar.activation(gT, bank[2][0:HID, :], ACT.Gelu, bias=L("fdb")[0:HID, :]))
                assert ch.count == ACT_LINKS, ch.count

        @block.vector
        def _(dve):
            V = nc.vector
            ch = Chain(dve, vset)

            def do(ins):
                ch.link(ins)
                ch.wait()

            dve.wait_ge(ld_c, 16 * 4)
            do(V.memset(small[:, 1:2], 1e-5))
            do(V.memset(small[:, 2:3], 1e-6))
            turns, r = small[:, 24:25], small[:, 18:19]
            magic = 1.5 * 2 ** 23
            do(V.tensor_scalar(turns, L("theta"), 0.15915494309189535, None, ALU.mult))
            do(V.tensor_scalar(turns, turns, magic, None, ALU.add))
            do(V.tensor_scalar(turns, turns, -magic, None, ALU.add))
            do(V.scalar_tensor_tensor(r, turns, -6.28125, L("theta"), ALU.mult, ALU.add))
            do(V.scalar_tensor_tensor(r, turns, -0.0019353071795864769, r, ALU.mult, ALU.add))
            do(V.tensor_scalar(r, r, -3.1415925, 3.1415925, ALU.max, ALU.min))
            do(V.tensor_scalar(small[:, 25:26], r, -1.0, None, ALU.mult))
            do(V.tensor_tensor(small[:, 25:26], small[:, 25:26], r, ALU.max))
            do(V.tensor_scalar(small[:, 19:20], small[:, 25:26], -1.0, 1.5707963267948966, ALU.mult, ALU.add))
            do(V.tensor_tensor(small[:, 44:52], L("lam", 0, 8), L("lam", 8, 16), ALU.mult))
            do(V.tensor_tensor(small[:, 52:60], L("lam", 16, 24), L("lam", 24, 32), ALU.mult))
            do(V.tensor_reduce(small[:, 22:24], small[:, 44:60].rearrange("p (a n) -> p a n", a=2), AX.X, ALU.add))
            V.nop().then_inc(su["trig_in"], 1)
            V.nop().then_inc(su["exp_in"], 1)
            do(V.tensor_scalar(small[:, 40:42], L("bproj", 8, 10), -1.0, None, ALU.mult))
            hi, mid, lo = bias_part
            do(V.tensor_copy(hi, bias_row))
            do(V.tensor_tensor(bias_rest, bias_row, hi, ALU.subtract))
            do(V.tensor_copy(mid, bias_rest))
            do(V.tensor_tensor(bias_rest, bias_rest, mid, ALU.subtract))
            do(V.tensor_copy(lo, bias_rest))
            V.nop().then_inc(su["split"], 1)
            do(V.memset(ones3[:, :], 1.0))
            do(V.memset(zc[:, :], 0.0))
            do(V.memset(state[:, :, :, :], 0.0))
            do(V.memset(fT[:, :, :, 0:2], 0.0))
            dve.wait_ge(su["trig"], 1)
            do(V.tensor_copy(sinT[:, 0:1], small[:, 16:17]))
            do(V.tensor_copy(cosT[:, 0:1], small[:, 17:18]))
            n = 1
            while n < TB:
                do(V.tensor_scalar(turns, sinT[:, n - 1:n], -1.0, None, ALU.mult))
                do(V.tensor_scalar(rota[:, 0:n], cosT[:, 0:n], cosT[:, n - 1:n], None, ALU.mult))
                do(V.tensor_scalar(rotb[:, 0:n], sinT[:, 0:n], cosT[:, n - 1:n], None, ALU.mult))
                do(V.scalar_tensor_tensor(cosT[:, n:2 * n], sinT[:, 0:n], turns, rota[:, 0:n], ALU.mult, ALU.add))
                do(V.scalar_tensor_tensor(sinT[:, n:2 * n], cosT[:, 0:n], sinT[:, n - 1:n], rotb[:, 0:n], ALU.mult, ALU.add))
                n *= 2
            do(V.tensor_scalar(sinT[:, :], sinT[:, :], C("sgn"), None, ALU.mult))
            dve.wait_ge(su["exp_out"], 1)
            do(V.tensor_tensor(turns, small[:, 20:21], small[:, 21:22], ALU.subtract))
            do(V.tensor_scalar(nlam, turns, -1.0, -LAMBDA_INIT, ALU.mult, ALU.add))
            ramp = flat(qkv[:, 0:3, :])[:, 0:1056]
            do(V.tensor_scalar(ramp, ramp, 1.0, None, ALU.add))
            do(V.reciprocal(ramp, ramp))
            do(V.scalar_tensor_tensor(dw, dw, L("condnorm"), ramp, ALU.mult, ALU.mult))
            do(V.tensor_scalar(W("wo"), W("wo"), L("outnorm"), None, ALU.mult))
            do(V.tensor_scalar(W("wp"), W("wp"), L("subln"), 1.0 - LAMBDA_INIT, ALU.mult, ALU.mult))
            dve.wait_ge(su["kv_sb"], 2)
            for h2 in range(2):
                for b in range(B):
                    do(V.tensor_tensor(kbx[:, h2, b, :].rearrange("p (h n) -> p h n", h=16),
                                       kn[:, 1, h2 * 256 + b * NK:h2 * 256 + b * NK + NK].unsqueeze(1).to_broadcast([P, 16, NK]),
                                       C("hh").unsqueeze(2).to_broadcast([P, 16, NK]), ALU.mult))
            vxv = vx[:, :, :, :].rearrange("p b h n -> p (b h) n")
            for f in range(2):
                do(V.tensor_scalar(vxv[:, :, 17 * f:17 * f + 16], M3[:, :, :], C("half")[:, f:f + 1], None, ALU.mult))
                do(V.tensor_copy(vxv[:, :, 17 * f + 16], C("half")[:, f:f + 1].to_broadcast([P, B * H])))
            dve.wait_ge(ld_b3, 48)
            do(V.memset(pre[:, :, :, 0:3], 0.0))
            V.nop().then_inc(su["ready"], 1)

            with dve.Fori(0, NI) as i:
                ch = Chain(dve, dchain, i, DVE_LINKS)

                def up(name, k=1):
                    dve.wait_ge(ev[name].sem, ev[name].at(i, k))

                def fin(name, ins):
                    ins.then_inc(ev[name].sem, 1)

                def own(ins):
                    ch.link(ins)
                    ch.wait()

                def landed():
                    V.memset(spare, 0.0)

                def bc(ap, n):
                    return ap.unsqueeze(2).to_broadcast([P, ap.shape[1], n])

                def layer_norm(src, dst, k, kn_):
                    for b in range(B):
                        last = V.bn_stats(stat[:, b, :], src[:, b, :])
                    own(last)
                    landed()
                    for b in range(B):
                        last = V.bn_aggr(mv[:, b, :], stat[:, b, :])
                    fin("var", last)
                    up("rstd", k)
                    for b in range(B):
                        last = V.tensor_scalar(dst[:, b, :], src[:, b, :], mv[:, b, 0:1], rstd[:, b:b + 1], ALU.subtract, ALU.mult)
                    fin("normed", last)

                dve.wait_ge(x_in.sem, x_in.at(i, 16))
                layer_norm(xt, hid, 1, 1)
                up("tr_ps", 1)
                fin("tr_v", V.tensor_copy(hT[:, 1, :], bank[1][:, :]))
                r3 = lambda ap: ap.rearrange("p (b t) -> p b t", b=B)
                cosb = cosT[:, :].unsqueeze(1).to_broadcast([P, B, TB])
                sinb = sinT[:, :].unsqueeze(1).to_broadcast([P, B, TB])
                up("rot_ps")
                V.tensor_tensor(r3(rota[:, :]), r3(bank[2][:, :]), cosb, ALU.mult)
                own(V.tensor_tensor(r3(rotb[:, :]), r3(bank[3][:, :]), sinb, ALU.mult))
                for b in range(B):
                    lo_, hi_ = b * TB, b * TB + TB
                    last = V.tensor_tensor_scan(qkv[:, 2, lo_:hi_], rota[:, lo_:hi_], rotb[:, lo_:hi_], zc[:, b:b + 1], ALU.add, ALU.add)
                fin("y", last)
                up("y2_ps")
                V.tensor_tensor(r3(rotb[:, :]), r3(bank[4][:, :]), sinb, ALU.mult)
                own(V.tensor_tensor(r3(rota[:, :]), r3(qkv[:, 2, :]), cosb, ALU.mult))
                fin("z", V.tensor_tensor(qkv[:, 0, :], rota[:, :], rotb[:, :], ALU.subtract))
                up("z")
                own(V.tensor_copy(zc[:, :], r3(qkv[:, 0, :])[:, :, TB - 1]))
                up("crs")
                fin("cond", V.tensor_tensor(rotb[:, :], qkv[:, 0, :], crs, ALU.mult))
                up("pre_sb", 2)
                bf = beta.rearrange("p g t -> p (g t)")
                own(V.tensor_scalar(bf, bf, 1.0, None, ALU.add))
                own(V.reciprocal(bf, bf))
                for j in range(6):
                    up("pre_sb", j + 3)
                    dst = r3(qkv[:, j, :])
                    own(V.tensor_scalar(dst, pre[:, j, :, 0:TB], L("conv", 4 * j, 4 * j + 1), None, ALU.mult))
                    for n in range(1, 4):
                        ins = V.scalar_tensor_tensor(dst, pre[:, j, :, n:TB + n], L("conv", 4 * j + n, 4 * j + n + 1), dst, ALU.mult, ALU.add)
                        if n < 3:
                            own(ins)
                        else:
                            fin("conv", ins)
                    V.tensor_copy(pre[:, j, :, 0:3], pre[:, j, :, TB:TB + 3])
                up("db_ps")
                d7 = bank[7][:, 0:B * 32].rearrange("p (b n) -> p b n", b=B)
                V.tensor_scalar(edb[:, :, 0:H], d7[:, :, 0:H], -43.0, None, ALU.max)
                fin("db_sb", V.tensor_scalar(edb[:, :, H:32], d7[:, :, H:32], -80.0, None, ALU.max))
                v3 = lambda ap: ap.rearrange("p (n t) -> p n t", t=CH)
                kqf = kq[:, :, :, :, :, :].rearrange("p g b c x t -> p g (b c) x t")
                for j in range(4):
                    up("rs", j + 1)
                    tmp = (M2, M4)[j % 2][:, 0:32, :]
                    if j < 2:
                        fin("qk_norm", V.tensor_tensor(kqf[:, j, :, 1, :], v3(qkv[:, j, :]), tmp, ALU.mult))
                    else:
                        own(V.tensor_tensor(v3(kn[:, j - 2, :]), v3(qkv[:, j, :]), tmp, ALU.mult))
                        fin("qk_norm", V.tensor_tensor(kqf[:, j - 2, :, 0, :], v3(kn[:, j - 2, :]), v3(beta[:, j - 2, :]), ALU.mult))
                up("db_exp")
                fin("db_one", V.tensor_scalar(edb[:, :, :], edb[:, :, :], 1.0, None, ALU.add))
                up("db_one")
                fin("bt", V.reciprocal(btc[:, :, :], edb[:, :, H:32]))
                up("act_silu", 6)
                m2b = M2b[:, :, :].rearrange("p n t -> p (n t)")
                m2w = m2b.rearrange("p (n w) -> p n w", w=32)
                for g in range(G):
                    last = V.transpose(m2b[:, g * 1024:g * 1024 + 1024],
                                       v3(qkv[:, 4 + g, :]).unsqueeze(2).to_broadcast([P, 32, 2, CH]))
                own(last)

                def half_select(dst):
                    own(V.tensor_scalar(dst, m2w[:, :, 0:16], C("dup")[:, 0:1], None, ALU.mult))
                    own(V.scalar_tensor_tensor(dst, m2w[:, :, 16:32], C("dup")[:, 1:2], dst, ALU.mult, ALU.add))

                half_select(vsel3)
                up("gsum_ps")
                for n, dst in enumerate((Gp, GCp, Bp)):
                    tmp = M3[:, :, :].rearrange("p n t -> p (n t)")[:, 0:512] if n % 2 else M3[:, :, :].rearrange("p n t -> p (n t)")[:, 512:1024]
                    t8 = tmp.rearrange("p (n h) -> p n h", h=HG)
                    own(V.tensor_tensor(t8, bank[n][:, :].rearrange("p (n h) -> p n h", h=HG), bd.unsqueeze(1).to_broadcast([P, NP_, HG]), ALU.mult))
                    own(V.tensor_reduce(dst, t8, AX.X, ALU.add))
                fin("gsel", V.tensor_tensor(eD, GCp, Gp, ALU.subtract))
                up("grow_ps")
                for n in range(2):
                    last = V.tensor_tensor(M2[:, 32 * n:32 * n + 32, :], bank[3 + n][:, :].rearrange("p (n t) -> p n t", t=CH),
                                           bc(Gp[:, 32 * n:32 * n + 32], CH), ALU.subtract)
                own(last)
                fin("d_ready", V.scalar_tensor_tensor(M2[:, :, :], M2[:, :, :], 0.0, C("neg").unsqueeze(1).to_broadcast([P, NP_, CH]), ALU.min, ALU.add))
                up("gexp")
                own(V.tensor_tensor(bG, Bp, eG, ALU.mult))
                pv = lambda ap: ap.rearrange("p (b g c) -> p b g c", b=B, g=G)
                mvw = lambda t: t[:, :, :].rearrange("p (b g c) t -> p b g c t", b=B, g=G)
                up("e_ready")
                for r in range(4):
                    up("raw_ps", 4 * r + 4)
                    g, c0 = r // 2, (r % 2) * 4
                    raw = bank[(0, 1, 2, 5)[r]][:, :].rearrange("p (c b x t) -> p c b x t", c=4, b=B, x=2)
                    e4 = mvw(M2)[:, :, g, c0:c0 + 4, :].rearrange("p b c t -> p c b t")
                    a4 = mvw(M3)[:, :, g, c0:c0 + 4, :].rearrange("p b c t -> p c b t")
                    m4 = mvw(M4)[:, :, g, c0:c0 + 4, :].rearrange("p b c t -> p c b t")
                    V.tensor_tensor(a4, raw[:, :, :, 0, :], e4, ALU.mult)
                    fin("am", V.tensor_tensor(m4, raw[:, :, :, 1, :], e4, ALU.mult))
                up("am", 4)
                for ph in range(2):
                    last = V.transpose(M5[:, :, :].rearrange("p (h t) s -> p t h s", h=4)[:, :, 2 * ph:2 * ph + 2, :],
                                       M3[:, 32 * ph:32 * ph + 32, :].rearrange("p k t -> p t k"))
                own(last)
                prod = M1[:, :, :].rearrange("p n t -> p (n t)")
                apr = M5[:, :, :].rearrange("p (h t) s -> p h t s", h=4)
                for t in range(1, CH):
                    pt_ = prod[:, 0:4 * t * t].rearrange("p (h j s) -> p h j s", h=4, j=t)
                    own(V.tensor_tensor(pt_, Tm[:, :, 0:t, 0:t], apr[:, :, t, 0:t].unsqueeze(2).to_broadcast([P, 4, t, t]), ALU.mult))
                    own(V.tensor_reduce(Tm[:, :, 0:t, t], pt_, AX.X, ALU.add, negate=True))
                for ph in range(2):
                    last = V.transpose(M3[:, 32 * ph:32 * ph + 32, :].rearrange("p k t -> p t k"),
                                       Tm[:, 2 * ph:2 * ph + 2, :, :].rearrange("p h j t -> p t (h j)"))
                fin("tinv", last)
                up("tinv")
                for g in range(G):
                    last = V.tensor_tensor(vb[:, g, :, :, :], vsel[:, g, :, :, :], pv(Bp)[:, :, g, :].unsqueeze(3).to_broadcast([P, B, NC, DH]), ALU.mult)
                own(last)

                def block_diag(s):
                    c, g = s // G, s % G
                    if s >= 2:
                        up("u_ps", s - 1)
                        up("ds_ps", s - 1)
                    for src, dst in ((M3, tbd), (M4, mbd)):
                        last = V.tensor_tensor(dst[:, s % 2, :, :].rearrange("p b (h t) -> p b h t", h=HG),
                                               mvw(src)[:, :, g, c, :].unsqueeze(2).to_broadcast([P, B, HG, CH]),
                                               bd.unsqueeze(1).unsqueeze(3).to_broadcast([P, B, HG, CH]), ALU.mult)
                    fin("tmbd", last)

                block_diag(0)
                for s in range(NSUB):
                    c, g = s // G, s % G
                    X = bank[(7, 3)[s % 2]]
                    xv = lambda n: X[:, 64 * n:64 * n + 64].rearrange("p (b v) -> p b v", b=B)
                    sm = lambda n: usm[:, s % 2, n, :].rearrange("p (b v) -> p b v", b=B)
                    col = lambda ap: pv(ap)[:, :, g, c].unsqueeze(2).to_broadcast([P, B, DH])
                    up("ks_ps", s + 1)
                    V.tensor_tensor(sm(0), xv(0), col(bG), ALU.mult)
                    own(V.tensor_tensor(sm(3), xv(1), col(eG), ALU.mult))
                    fin("r_ready", V.tensor_tensor(sm(0), vb[:, g, :, c, :], sm(0), ALU.subtract))
                    own(V.tensor_tensor(state[:, :, g, :], state[:, :, g, :], col(eGC), ALU.mult))
                    if s + 1 < NSUB:
                        block_diag(s + 1)
                    up("u_ps", s + 1)
                    V.tensor_copy(sm(1), xv(2))
                    fin("u_sb", V.tensor_tensor(sm(2), xv(2), col(eD), ALU.mult))
                    up("ds_ps", s + 1)
                    V.tensor_tensor(state[:, :, g, :], state[:, :, g, :], xv(3), ALU.add)
                    fin("s_new", V.tensor_tensor(obuf[:, g, :, :].rearrange("p (b c) v -> p b c v", b=B)[:, :, c, :], xv(4), sm(3), ALU.add))
                up("osq")
                fin("osum", V.tensor_reduce(ors, M2[:, :, :], AX.X, ALU.add))
                up("ors")
                og3 = M1[:, :, :]
                own(V.tensor_tensor(og3, og3, bc(ors, DH), ALU.mult))
                for g in range(G):
                    last = V.transpose(m2b[:, g * 1024:g * 1024 + 1024], obuf[:, g, :, :].unsqueeze(2).to_broadcast([P, 32, 2, DH]))
                own(last)
                kn3 = kn[:, :, :].rearrange("p g (n t) -> p (g n) t", t=CH)
                half_select(kn3)
                fin("og", V.tensor_tensor(flat(kn[:, :, :]), flat(kn[:, :, :]), flat(sg[:, :, :]), ALU.mult))

                def add_residual(name, banks):
                    up(name)
                    for n, bk in enumerate(banks):
                        half_ = flat(xt[:, 2 * n:2 * n + 2, :])
                        last = V.tensor_tensor(half_, bank[bk][:, :], half_, ALU.add)
                    own(last)

                add_residual("wo_ps", (0, 1))
                layer_norm(xt, n2, 2, 2)
                up("tr_ps", 2)
                fin("tr_v", V.tensor_copy(n2T[:, 1, :], bank[1][:, :]))
                mx = pk[:, 0, 0:16].rearrange("p (f h) -> p f h", f=2)
                rr = pk[:, 1, 0:16].rearrange("p (h f) -> p h f", f=2)
                ta = M1[:, 0:16, :]
                for u in range(8):
                    b, hc = u // 2, u % 2
                    up("sc_ps", u + 1)
                    sc = [bank[4 + f][:, :].rearrange("p (h n) -> p h n", h=8) for f in range(2)]
                    for f in range(2):
                        last = V.tensor_reduce(mx[:, f, :], sc[f], AX.X, ALU.max)
                    own(last)
                    if u:
                        up("pt_ps", u)
                    for f in range(2):
                        last = V.tensor_tensor(prob[:, :, f, :], sc[f], bc(mx[:, f, :], NK), ALU.subtract)
                    fin("psub", last)
                    up("pt_ps", u + 1)
                    fin("pt_v", V.tensor_copy(probT[:, 4:8, :].rearrange("p h t -> p (h t)"), bank[6][:, :]))
                    up("pv_ps", u + 1)
                    ov = bank[7][:, 0:272].rearrange("p (h f n) -> p h f n", h=8, f=2)
                    own(V.reciprocal(rr, ov[:, :, :, 16]))
                    own(V.tensor_scalar(rr[:, :, 1], rr[:, :, 1], nlam, None, ALU.mult))
                    own(V.tensor_tensor(ta, bank[7][:, 0:272].rearrange("p (h n) -> p h n", n=17)[:, :, 0:16],
                                        pk[:, 1, 0:16].unsqueeze(2).to_broadcast([P, 16, 16]), ALU.mult))
                    tav = ta.rearrange("p (h f) v -> p h f v", f=2)
                    fin("a_sb", V.tensor_tensor(ax[:, b, 8 * hc:8 * hc + 8, :], tav[:, :, 0, :], tav[:, :, 1, :], ALU.add))
                up("asq")
                fin("asum", V.tensor_reduce(ors, at2.rearrange("p (n v) -> p n v", v=DH), AX.X, ALU.add))
                up("ars")
                ax3 = ax.rearrange("p b h v -> p (b h) v")
                fin("normed", V.tensor_tensor(ax3, ax3, bc(ors, DH), ALU.mult))
                up("tr_ps", 3)
                fin("tr_v", V.tensor_copy(n2T[:, 1, :], bank[1][:, :]))
                add_residual("wp_ps", (2, 3))

                layer_norm(xt, n2, 3, 4)
                up("tr_ps", 4)
                fin("tr_v", V.tensor_copy(fT[:, 1, :, 2:TB + 2], r3(bank[1][:, :])))
                up("tr_v", 4)
                up("tr_a", 4)
                for k in range(KC):
                    dst = r3(dcv[:, k, :])
                    own(V.tensor_scalar(dst, fT[:, k, :, 0:TB], L("dwk", 3 * k, 3 * k + 1), L("dwb", k, k + 1), ALU.mult, ALU.add))
                    own(V.scalar_tensor_tensor(dst, fT[:, k, :, 1:TB + 1], L("dwk", 3 * k + 1, 3 * k + 2), dst, ALU.mult, ALU.add))
                    last = V.scalar_tensor_tensor(dst, fT[:, k, :, 2:TB + 2], L("dwk", 3 * k + 2, 3 * k + 3), dst, ALU.mult, ALU.add)
                fin("dconv", last)
                V.tensor_copy(fT[:, :, :, 0:2], fT[:, :, :, TB:TB + 2])
                up("pws")
                for k in range(KC):
                    last = V.tensor_tensor(r3(x1T[:, k, :]), r3(sT[:, k, :]), fT[:, k, :, 2:TB + 2], ALU.add)
                fin("x1T", last)
                up("lgt_ps")
                own(V.tensor_copy(rwt[:, 0, :, :], bank[2][:, 0:32].rearrange("p (b e) -> p b e", b=B)))
                landed()
                for b in range(B):
                    last = V.max(rwt[:, 1, b, :], rwt[:, 0, b, :])
                own(last)
                landed()
                for b in range(B):
                    V.max_index(idx[:, b, :], rwt[:, 1, b, :], rwt[:, 0, b, :])
                own(V.tensor_tensor(rwt[:, 3, :, 0], rwt[:, 1, :, 1], rwt[:, 1, :, 0], ALU.subtract))
                fin("top", V.tensor_copy(rwt[:, 2, :, :], idx[:, :, :]))
                up("texp")
                own(V.tensor_scalar(rwt[:, 3, :, 2], rwt[:, 3, :, 1], 1.0, None, ALU.add))
                own(V.reciprocal(rwt[:, 3, :, 3], rwt[:, 3, :, 2]))
                own(V.tensor_tensor(rwt[:, 3, :, 4], rwt[:, 3, :, 1], rwt[:, 3, :, 3], ALU.mult))
                for n in range(2):
                    own(V.tensor_tensor(rwt[:, 4 + n, :, :], C("iota").unsqueeze(1).to_broadcast([P, B, NE]), bc(rwt[:, 2, :, n], NE), ALU.is_equal))
                    own(V.tensor_tensor(rwt[:, 4 + n, :, :], rwt[:, 4 + n, :, :], bc(rwt[:, 3, :, 3 + n], NE), ALU.mult))
                own(V.tensor_tensor(rwt[:, 6, :, :], rwt[:, 4, :, :], rwt[:, 5, :, :], ALU.add))
                for u in range(16):
                    b, ep = u // 4, u % 4
                    up("moe_act", u + 1)
                    for e2 in range(2):
                        e = 2 * ep + e2
                        src, wgt = ye[:, u % 4, e2 * D:e2 * D + D], rwt[:, 6, b, e:e + 1]
                        if e == 0:
                            ins = V.tensor_scalar(comb[:, b, :], src, wgt, None, ALU.mult)
                        else:
                            ins = V.scalar_tensor_tensor(comb[:, b, :], src, wgt, comb[:, b, :], ALU.mult, ALU.add)
                        if e2:
                            fin("moe_acc", ins)
                            up("moe_acc", u + 1)
                        else:
                            own(ins)
                up("tr_ps", 5)
                fin("tr_v", V.tensor_copy(combT[:, 1, :], bank[1][:, :]))
                up("mo_ps")
                for n in range(2):
                    last = V.tensor_copy(flat(hx[:, 2 * n:2 * n + 2, :]), bank[2 + n][:, :])
                fin("mo_sb", last)
                up("hrs")
                for b in range(B):
                    last = V.scalar_tensor_tensor(hx[:, b, :], hx[:, b, :], rstd[:, b:b + 1], W("normw"), ALU.mult, ALU.mult)
                fin("hn", last)
                up("tr_ps", 6)
                fin("tr_v", V.tensor_copy(hTT[:, 1, :], bank[1][:, :]))
                up("xh")
                up("ffu_ps")
                for n in range(2):
                    last = V.tensor_tensor(flat(ot[:, 2 * n:2 * n + 2, :]), bank[4 + n][:, :], flat(xt[:, 2 * n:2 * n + 2, :]), ALU.add)
                fin("done", last)
                assert ch.count == DVE_LINKS, ch.count

        @block.tensor
        def _(pe):
            mm = nc.tensor.matmul

            def over_k(dst, lhs, rhs, n=KC):
                for k in range(n):
                    last = mm(dst, lhs(k), rhs(k), start=k == 0, stop=k == n - 1)
                return last

            pe.wait_ge(ld_w, 16 * 6)
            wk_, wv_ = [hT[:, n, :].rearrange("p (k n) -> p k n", k=KC) for n in range(2)]
            ctx_ = kn[:, 0, :].rearrange("p (k n) -> p k n", k=KC)
            ctxd_ = flat(xt[:, :, :]).rearrange("p (k b n) -> p k b n", k=KC, b=B)
            for h2 in range(2):
                last = over_k(bank[h2][:, 0:256], lambda k: wk_[:, k, h2 * P:h2 * P + P], lambda k: ctx_[:, k, :])
            last.then_inc(su["kproj"], 1)
            for b in range(B):
                last = over_k(bank[2 + b // 2][:, (b % 2) * D:(b % 2) * D + D], lambda k: ctxd_[:, k, b, :], lambda k: wv_[:, k, :])
            last.then_inc(su["vproj"], 1)
            pe.wait_ge(su["ready"], 1)

            with pe.Fori(0, NI) as i:
                def up(name, k=1):
                    pe.wait_ge(ev[name].sem, ev[name].at(i, k))

                def fin(name, ins):
                    ins.then_inc(ev[name].sem, 1)

                def bias(dst, name, a=0, b=None, stop=True):
                    lo_, hi_ = BOFF[name]
                    return mm(dst, ones3[:, :], bias3[:, lo_ + a:(hi_ if b is None else lo_ + b)], start=False, stop=stop)

                def turn(src, name):
                    for k in range(KC):
                        for b in range(B):
                            last = nc.tensor.transpose(bank[k][:, b * TB:b * TB + TB], src[:, b, k * P:k * P + P], ident)
                    fin("tr_ps", last)

                def turned(k):
                    up("tr_a", k)
                    up("tr_v", k)

                up("normed", 1)
                turn(hid, 1)
                turned(1)
                for n in range(2):
                    last = over_k(bank[2 + n][:, :], lambda k: cin[:, k, n * P:n * P + P], lambda k: hT[:, k, :])
                fin("rot_ps", last)
                up("y")
                fin("y2_ps", mm(bank[4][:, :], C("swap"), qkv[:, 2, :], start=True, stop=True))
                up("zsq")
                fin("zsum_ps", mm(bank[5][:, :], C("ones"), qkv[:, 1, :], start=True, stop=True))
                up("cond")
                for j in range(10):
                    if j >= 4:
                        up("pre_sb", j - 3)
                    cc = 1024 + j * P if j < 2 else (j - 2) * P
                    dst = bank[j % 4][:, :]
                    for k in range(KC):
                        last = mm(dst, ctrl[:, k, cc:cc + P], hT[:, k, :], start=k == 0, stop=j >= 8 and k == 1)
                    if j < 8:
                        dc = 768 + j * P if j < 2 else (j - 2) * P
                        last = mm(dst, dw[:, dc:dc + P], rotb[:, :], start=False, stop=True)
                    fin("proj_ps", last)
                for b in range(B):
                    dst = bank[7][:, b * 32:b * 32 + 32]
                    for k in range(KC):
                        mm(dst, hT[:, k, b * TB:b * TB + TB], ctrl[:, k, 1280:1312], start=k == 0, stop=False)
                    mm(dst, rotb[:, b * TB:b * TB + TB], dw[:, 1024:1056], start=False, stop=False)
                    last = bias(dst, "db")
                fin("db_ps", last)
                for j in range(4):
                    up("sq", j + 1)
                    if j >= 2:
                        up("rs", j - 1)
                    fin("sum_ps", mm(bank[4 + j % 2][:, :], C("bones"), (rota, rotb)[j % 2][:, :], start=True, stop=True))
                up("xpand", 2)
                up("pre_sb", 10)
                mm(bank[0][:, :], C("tri"), rota[:, :], start=True, stop=True)
                mm(bank[1][:, :], C("negones"), rota[:, :], start=True, stop=True)
                fin("gsum_ps", mm(bank[2][:, :], C("delta"), rotb[:, :], start=True, stop=True))
                up("lrep")
                lrep = M1[:, :, :].rearrange("p n t -> p (n t)")
                for n in range(B * G):
                    last = mm(bank[3 + n // 4][:, (n % 4) * P:(n % 4) * P + P], lrep[:, n * P:n * P + P], C("triblk"), start=True, stop=True)
                fin("grow_ps", last)
                up("gsel")
                for s in range(NSUB):
                    g, c = s // NC, s % NC
                    up("kbd", s + 1)
                    for b in range(B):
                        at = (s % 4) * P + b * 2 * CH
                        last = mm(bank[(0, 1, 2, 5)[s // 4]][:, at:at + 2 * CH], kbd[:, s % 2, b, :],
                                  kq[:, g, b, c, :, :].rearrange("p x t -> p (x t)"), start=True, stop=True)
                    fin("raw_ps", last)

                def old_state(s):
                    g, X = s % G, bank[(7, 3)[s % 2]]
                    up("kbd", NSUB + s + 1)
                    up("qbd", s + 1)
                    if s:
                        up("kt_sb", s)
                    for b in range(B):
                        last = nc.tensor.transpose(bank[6][:, b * P:b * P + P], kbd[:, s % 2, b, :], ident)
                    fin("kt_ps", last)
                    if s >= 2:
                        up("s_new", s - 1)
                    for n, src in enumerate((kbd, qbd)):
                        for b in range(B):
                            last = mm(X[:, 64 * n + DH * b:64 * n + DH * b + DH], src[:, s % 2, b, :], state[:, b, g, :], start=True, stop=True)
                    fin("ks_ps", last)

                up("d_ready")
                old_state(0)
                for s in range(NSUB):
                    X = bank[(7, 3)[s % 2]]
                    if s + 1 < NSUB:
                        old_state(s + 1)
                    up("tmbd", s + 1)
                    up("r_ready", s + 1)
                    for b in range(B):
                        last = mm(X[:, 128 + DH * b:128 + DH * b + DH], tbd[:, s % 2, b, :], usm[:, s % 2, 0, DH * b:DH * b + DH], start=True, stop=True)
                    fin("u_ps", last)
                    up("u_sb", s + 1)
                    up("kt_sb", s + 1)
                    for n, lhs, src in ((3, ktb, 2), (4, mbd, 1)):
                        for b in range(B):
                            last = mm(X[:, 64 * n + DH * b:64 * n + DH * b + DH], lhs[:, s % 2, b, :], usm[:, s % 2, src, DH * b:DH * b + DH], start=True, stop=True)
                    fin("ds_ps", last)

                def to_tokens(dst0, lhs, rhs, name):
                    for b in range(B):
                        dst = bank[dst0 + b // 2][:, (b % 2) * D:(b % 2) * D + D]
                        for k in range(KC):
                            mm(dst, lhs[:, k, b * TB:b * TB + TB], rhs[:, k, :], start=k == 0, stop=False)
                        last = bias(dst, name)
                    return last

                up("og")
                fin("wo_ps", to_tokens(0, kn, wo, "wo"))

                up("normed", 2)
                turn(n2, 2)
                turned(2)
                for n in range(2):
                    last = over_k(bank[2 + n][:, :], lambda k: wq[:, k, n * P:n * P + P], lambda k: n2T[:, k, :])
                fin("qx_ps", last)
                up("qx_sb")

                def scores(u):
                    b, hc = u // 2, u % 2
                    if u:
                        up("psub", u)
                    for f in range(2):
                        last = mm(bank[4 + f][:, :], qx[:, f, b * TB:b * TB + TB], kbx[:, f, b, hc * 512:hc * 512 + 512], start=True, stop=True)
                    fin("sc_ps", last)

                scores(0)
                for u in range(8):
                    b, hc = u // 2, u % 2
                    if u < 7:
                        scores(u + 1)
                    up("pexp", u + 1)
                    if u:
                        up("pt_a", u)
                        up("pt_v", u)
                    for h in range(8):
                        last = nc.tensor.transpose(bank[2 if h < 4 else 6][:, (h % 4) * P:(h % 4) * P + P],
                                                   prob[:, h, :, :].rearrange("p f n -> p (f n)"), ident)
                    fin("pt_ps", last)
                    up("pt_a", u + 1)
                    up("pt_v", u + 1)
                    if u:
                        up("a_sb", u)
                    for h in range(8):
                        last = mm(bank[7][:, 34 * h:34 * h + 34], probT[:, h, :], vx[:, b, 8 * hc + h, :], start=True, stop=True)
                    fin("pv_ps", last)
                up("normed", 3)
                turn(ax.rearrange("p b h v -> p b (h v)"), 3)
                turned(3)
                fin("wp_ps", to_tokens(2, n2T, wp, "xp"))

                up("normed", 4)
                turn(n2, 4)
                up("dconv")
                for n in range(2):
                    last = over_k(bank[2 + n][:, :], lambda k: pw[:, k, n * P:n * P + P], lambda k: dcv[:, k, :])
                fin("pw_ps", last)
                up("x1T")
                for b in range(B):
                    dst = bank[2][:, b * NE:b * NE + NE]
                    for k in range(KC):
                        mm(dst, x1T[:, k, b * TB:b * TB + TB], rw_w[:, k, :], start=k == 0, stop=False)
                    last = bias(dst, "router")
                fin("lgt_ps", last)
                for u in range(16):
                    b, ep = u // 4, u % 4
                    if u >= 4:
                        up("moe_act", u - 3)
                    dst = bank[4 + u % 4][:, :]
                    for k in range(KC):
                        mm(dst, x1T[:, k, b * TB:b * TB + TB], ew[:, k, ep * 512:ep * 512 + 512], start=k == 0, stop=False)
                    fin("moe_ps", bias(dst, "e", ep * 512, ep * 512 + 512))
                up("moe_acc", 16)
                turn(comb, 5)
                turned(5)
                for b in range(B):
                    dst = bank[2 + b // 2][:, (b % 2) * D:(b % 2) * D + D]
                    for k in range(KC):
                        mm(dst, combT[:, k, b * TB:b * TB + TB], ow[:, k, :], start=k == 0, stop=False)
                    for k in range(KC):
                        mm(dst[:, k * P:k * P + P], x1T[:, k, b * TB:b * TB + TB], ident, start=False, stop=False)
                    last = bias(dst, "out")
                fin("mo_ps", last)
                up("hn")
                turn(hx, 6)
                turned(6)
                fin("ffd_ps", over_k(bank[2][0:HID, :], lambda k: ffd[:, k, :], lambda k: hTT[:, k, :]))
                up("gelu")
                for b in range(B):
                    dst = bank[4 + b // 2][:, (b % 2) * D:(b % 2) * D + D]
                    mm(dst, gT[:, b * TB:b * TB + TB], ffu, start=True, stop=False)
                    last = bias(dst, "up")
                fin("ffu_ps", last)


def layout(v):
    import numpy as np

    def chunks(w):
        return np.concatenate([w[:P], w[P:]], axis=1)

    def both(w):
        return w.reshape(KC, P).T

    reim = np.concatenate([np.arange(0, P, 2), np.arange(1, P, 2)])
    imre = np.concatenate([np.arange(1, P, 2), np.arange(0, P, 2)])
    zeros = lambda *s: np.zeros(s, np.float32)
    cin = v["L0_attn_cond_in_W"]
    dW = v["L0_attn_delta_W"][reim]
    cW, cb = v["L0_attn_ctrl_W"], v["L0_attn_ctrl_b"]
    dec, bet, gate = slice(768, 784), slice(784, 800), slice(800, 1056)
    rep = lambda a: np.repeat(a, DH, axis=-1)
    ctrl = np.concatenate([cW[:, :768], cW[:, gate], rep(cW[:, bet]), cW[:, dec], cW[:, bet]], axis=1)
    ew = v["L0_ffn_expert_w"].transpose(2, 0, 1).reshape(D, NE * D)
    parts = {
        "cin": chunks(np.concatenate([cin[:, reim], cin[:, imre]], axis=1)),
        "dw": np.concatenate([dW[:, :768], rep(dW[:, 768:784]), zeros(P, 16), dW[:, 768:784]], axis=1),
        "ctrl": chunks(ctrl), "wo": chunks(v["L0_attn_out_proj_W"].T), "wq": chunks(v["L0_xattn_Wq"].T),
        "wp": chunks(v["L0_xattn_Wp"].T), "pw": chunks(v["L0_ffn_pw_w"].T), "rw": chunks(v["L0_ffn_router_w"].T),
        "ew": chunks(ew), "ow": chunks(v["L0_ffn_out_w"].T), "normw": np.broadcast_to(v["L0_ffn_norm_w"], (P, D)),
        "ffd": chunks(v["L0_ffn_ff_down_w"].T), "ffu": np.concatenate([v["L0_ffn_ff_up_w"].T, zeros(HID, D)], axis=0)}
    weights = np.concatenate([parts[n] for n, _ in WEIGHTS], axis=1)

    p = np.arange(P)
    hp, tp = p // CH, p % CH
    f = lambda a: np.asarray(a, np.float32)
    same_t = tp[:, None] == tp[None, :]
    con = {
        "ident": f(np.eye(P)), "swap": f(np.eye(P)[np.concatenate([p[64:], p[:64]])]), "ones": f(np.ones((P, P))),
        "bones": f(hp[:, None] == hp[None, :]), "tri": -f(tp[:, None] <= tp[None, :]), "negones": -f(np.ones((P, P))),
        "delta": f(same_t), "triblk": -f((hp[:, None] == hp[None, :]) & (tp[:, None] <= tp[None, :])),
        "bd": f(hp[:, None] == np.arange(HG)), "mc": f(hp[:, None] == np.arange(NC)),
        "neg": f(np.where(np.arange(CH)[None, :] >= tp[:, None], 0.0, -1e30)), "hh": f((p // 8)[:, None] == np.arange(16)),
        "half": f((p // 64)[:, None] == np.arange(2)), "iota": f(np.broadcast_to(np.arange(NE), (P, NE))),
        "sgn": f(np.where(p < 64, 1.0, -1.0))[:, None], "dup": f((hp % 2)[:, None] == np.arange(2))}
    consts = np.concatenate([con[n] for n, _ in CONSTS], axis=1)

    conv = np.concatenate([v[f"L0_attn_{n}_conv_w"].reshape(KC, P, 4).transpose(1, 0, 2).reshape(P, 8) for n in "qkv"], axis=1)
    col = {
        "bproj": np.concatenate([cb[:768].reshape(6, P).T, both(cb[gate]), both(rep(cb[bet]))], axis=1),
        "conv": conv, "theta": np.tile(v["L0_attn_rot_theta"], 2)[:, None], "condnorm": v["L0_attn_cond_norm_w"][reim][:, None],
        "outnorm": np.tile(v["L0_attn_out_norm_w"], 8)[:, None], "subln": np.tile(v["L0_xattn_subln_w"], 8)[:, None],
        "pwb": both(v["L0_ffn_pw_b"]), "dwk": v["L0_ffn_dw_kernel"][:, 0, :].reshape(KC, P, 3).transpose(1, 0, 2).reshape(P, 6),
        "dwb": both(v["L0_ffn_dw_bias"]), "fdb": np.concatenate([v["L0_ffn_ff_down_b"], zeros(HID)])[:, None],
        "lam": np.broadcast_to(np.concatenate([v[f"L0_xattn_{n}"] for n in ("lq1", "lk1", "lq2", "lk2")]), (P, 32))}
    cols = np.concatenate([col[n] for n, _ in COLUMNS], axis=1)

    ramp = np.concatenate([v["L0_attn_qkv_ramp_logit"].reshape(768), rep(v["L0_attn_beta_ramp_logit"]), zeros(16), v["L0_attn_beta_ramp_logit"]])
    cT = v["ctx_1024"].transpose(2, 0, 1)
    scr = {
        "ramp": np.broadcast_to(ramp, (P, 1056)), "wk": chunks(v["L0_xattn_Wk"].T), "wv": chunks(v["L0_xattn_Wv"].T),
        "ctx": chunks(cT.reshape(D, B * NK)), "ctxd": chunks(np.concatenate([cT, cT], axis=2).reshape(D, B * 2 * NK))}
    scratch = np.concatenate([scr[n] for n, _ in SCRATCH], axis=1)

    bia = {"e": v["L0_ffn_expert_b"].reshape(-1), "out": v["L0_ffn_out_b"], "wo": v["L0_attn_out_proj_b"], "xp": v["L0_xattn_bp"],
           "up": v["L0_ffn_ff_up_b"], "router": v["L0_ffn_router_b"], "db": np.concatenate([cb[dec], cb[bet]])}
    biases = np.concatenate([bia[n] for n, _ in BIASES])[None, :]
    teye = f(np.tile(np.eye(CH).reshape(1, CH * CH), (P, 4)))
    return {"in_x": v["x"], "in_weights": weights, "in_consts": consts, "in_cols": cols, "in_scratch": scratch,
            "in_biases": biases, "in_teye": teye}


def kernel(**inputs):
    import numpy as np
    import concourse.bacc as bacc
    from concourse.bass_utils import run_bass_kernel_spmd as run

    nc = bacc.Bacc("TRN2", target_bir_lowering=False, num_devices=1)
    arrays = {n: np.ascontiguousarray(a) for n, a in layout({n: np.asarray(a) for n, a in inputs.items()}).items()}
    args = [nc.dram_tensor(n, a.shape, F32, kind="ExternalInput").ap() for n, a in arrays.items()]
    out = nc.dram_tensor("out_0", (B, S, D), F32, kind="ExternalOutput").ap()
    build(nc, args[0], out, *args[1:])
    r = run(nc, [arrays], core_ids=[0])
    return r.results[0]["out_0"]
```

```python
from contextlib import ExitStack

import concourse.bass as bass
from concourse import mybir

F32 = mybir.dt.float32
BF16 = mybir.dt.bfloat16
U32 = mybir.dt.uint32
ACT = mybir.ActivationFunctionType
ALU = mybir.AluOpType
AX = mybir.AxisListType

P = 128
B, S, D = 4, 1024, 256
H, DH = 16, 16
NK = 64
NE, HID = 8, 64
KC = D // P
TB = P
T = B * TB
NI = S // TB
CH = 16
NC = TB // CH
G = 2
HG = H // G
NP_ = B * G * NC
NSUB = NC * G
LAMBDA_INIT = 0.8 - 0.6 * 2.718281828459045 ** (-0.3 * 4)
XSCALE = 8 ** -0.5

WEIGHTS = [("cin", KC * 256), ("dw", 1056), ("ctrl", KC * 1312), ("wo", KC * D), ("wq", KC * D), ("wp", KC * D),
           ("pw", KC * D), ("rw", KC * NE), ("ew", KC * NE * D), ("ow", KC * D), ("normw", D),
           ("ffd", KC * HID), ("ffu", D)]
CONSTS = [("ident", P), ("swap", P), ("ones", P), ("bones", P), ("tri", P), ("negones", P), ("delta", P),
          ("triblk", P), ("bd", HG), ("mc", NC), ("neg", CH), ("hh", 8), ("half", 2), ("iota", NE), ("sgn", 1), ("dup", 2)]
COLUMNS = [("bproj", 10), ("conv", 24), ("theta", 1), ("condnorm", 1), ("outnorm", 1), ("subln", 1),
           ("pwb", 2), ("dwk", 6), ("dwb", 2), ("fdb", 1), ("lam", 32)]
SCRATCH = [("ramp", 1056), ("wk", KC * D), ("wv", KC * D), ("ctx", KC * B * NK), ("ctxd", KC * B * 2 * NK)]
BIASES = [("e", NE * D), ("out", D), ("wo", D), ("xp", D), ("up", D), ("router", NE), ("db", 32)]


def offsets(parts):
    at, out = 0, {}
    for name, size in parts:
        out[name] = (at, at + size)
        at += size
    return out, at


WOFF, NW = offsets(WEIGHTS)
COFF, NCON = offsets(CONSTS)
LOFF, NCOL = offsets(COLUMNS)
SOFF, NSCR = offsets(SCRATCH)
BOFF, NBIAS = offsets(BIASES)


class Event:

    def __init__(self, sem, per=1):
        self.sem, self.per = sem, per

    def at(self, i, k=1):
        return i * self.per + k


class Chain:

    def __init__(self, eng, sem, i=0, per=0):
        self.eng, self.sem, self.i, self.per, self.count = eng, sem, i, per, 0

    def link(self, ins):
        self.count += 1
        ins.then_inc(self.sem, 1)
        return self.count

    def wait(self, step=None):
        step = self.count if step is None else step
        self.eng.wait_ge(self.sem, self.i * self.per + step if self.per else step)

    def do(self, ins):
        self.link(ins)
        self.wait()


DVE_AB, DVE_CD, ACT_AB, ACT_CD = 102, 74, 8, 6

FIRST_HALF = {"ln1", "turn1", "rot", "unrot", "cond", "proj", "beta", "conv", "silu", "db", "sum", "decay", "spread", "grow",
              "raw", "am", "solve", "vpack", "bd", "old", "u", "new", "onorm", "wo", "x1"}
ORDER = ([("ln1",), ("ln2",), ("turn1",), ("rot",), ("turn2",), ("sc", 0), ("unrot",), ("max", 0), ("cond",)]
         + [("proj", 0), ("proj", 1), ("beta",), ("pt", 0), ("proj", 2), ("proj", 3), ("av", 0), ("max", 1), ("proj", 4)]
         + [("conv", 0), ("pt", 1), ("proj", 5), ("proj", 6), ("av", 1), ("max", 2), ("conv", 1), ("pt", 2), ("proj", 7), ("db",)]
         + [("av", 2), ("max", 3), ("conv", 2), ("proj", 8), ("proj", 9), ("pt", 3), ("silu",), ("av", 3), ("max", 4), ("sum", 0), ("sum", 1), ("pt", 4)]
         + [("sum", 2), ("sum", 3), ("av", 4), ("max", 5), ("spread",), ("raw", 0), ("decay",), ("pt", 5), ("grow",), ("av", 5), ("max", 6), ("raw", 1)]
         + [("pt", 6), ("raw", 2), ("raw", 3), ("av", 6), ("max", 7), ("am",), ("pt", 7), ("vpack",), ("av", 7), ("anorm",), ("solve", 0), ("wp",), ("solve", 1)]
         + [("ln3",), ("solve", 2), ("turn4",), ("dconv",), ("pw",), ("solve", 3), ("router",), ("top",), ("bd", 0), ("old", 0)]
         + [step for s in range(16) for step in ([("old", s + 1)] if s < 15 else []) + [("moe", s), ("u", s)]
            + ([("bd", s + 1)] if s < 15 else []) + [("acc", s), ("new", s)]]
         + [("turn5",), ("onorm",), ("mo",), ("hnorm",), ("wo",), ("turn6",), ("ffn",), ("x1",)])


def build(nc, x, out, weights, consts, cols, scratch, biases, teye, dbg=None):
    ctx = ExitStack()
    with ctx:
        def sb(name, shape, dt=F32):
            return ctx.enter_context(nc.sbuf_tensor(name, shape, dt))

        def sem(name):
            return ctx.enter_context(nc.semaphore(name))

        def event(name, per=1):
            return Event(sem(name), per)

        bank = [ctx.enter_context(nc.psum_tensor(f"bank{n}", [P, 512], F32)) for n in range(8)]

        w_sb = sb("w_sb", [P, NW])
        c_sb = sb("c_sb", [P, NCON])
        l_sb = sb("l_sb", [P, NCOL])

        def W(name):
            return w_sb[:, WOFF[name][0]:WOFF[name][1]]

        def C(name):
            return c_sb[:, COFF[name][0]:COFF[name][1]]

        def L(name, a=0, b=None):
            lo, hi = LOFF[name]
            return l_sb[:, lo + a:(hi if b is None else lo + b)]

        cin = W("cin").rearrange("p (k n) -> p k n", k=KC)
        ctrl = W("ctrl").rearrange("p (k n) -> p k n", k=KC)
        wo = W("wo").rearrange("p (k n) -> p k n", k=KC)
        wq = W("wq").rearrange("p (k n) -> p k n", k=KC)
        wp = W("wp").rearrange("p (k n) -> p k n", k=KC)
        pw = W("pw").rearrange("p (k n) -> p k n", k=KC)
        rw_w = W("rw").rearrange("p (k n) -> p k n", k=KC)
        ew = W("ew").rearrange("p (k n) -> p k n", k=KC)
        ow = W("ow").rearrange("p (k n) -> p k n", k=KC)
        ffd = W("ffd").rearrange("p (k n) -> p k n", k=KC)
        ffu = W("ffu")[0:HID, :]
        dw = W("dw")
        ident = C("ident")
        bd = C("bd")
        cosT = sb("cosT", [P, TB])
        sinT = sb("sinT", [P, TB])
        small = sb("small", [P, 64])
        bias3 = sb("bias3", [3, NBIAS], BF16)
        ones3 = sb("ones3", [3, P], BF16)
        kbx = sb("kbx", [P, 2, B, 8 * NK])
        vx = sb("vx", [P, B, H, 34])
        nlam, eps5, eps6, one, spare = [small[:, n:n + 1] for n in range(5)]
        negb = small[:, 40:42]
        bw3 = small[:, 26:32]

        zc = sb("zc", [P, B])
        state = sb("state", [P, B, G, DH])
        halo = sb("halo", [P, 6, B, 3])
        fT = sb("fT", [P, KC, B, TB + 2])

        xt = sb("xt", [P, B, D])
        hid = sb("hid", [P, B, D])
        hT = sb("hT", [P, KC, T])
        qkv = sb("qkv", [P, 6, T])
        rota = sb("rota", [P, T])
        rotb = sb("rotb", [P, T])
        kn = sb("kn", [P, G, T])
        kq = sb("kq", [P, G, B, NC, 2, CH])
        sg = sb("sg", [P, G, T])
        stat = sb("stat", [P, 2, B, 6])
        mv = sb("mv", [P, 2, B, 2])
        rstd = sb("rstd", [P, 2, B])
        edb = sb("edb", [P, B, 32])
        lgc = sb("lgc", [P, B, H])
        btc = sb("btc", [P, B, H])
        pk = sb("pk", [P, 8, NP_])
        Gp, GCp, Bp, eG, eGC, eD, bG, ors = [pk[:, n, :] for n in range(8)]
        M1, M2, M3, M4, M5 = [sb(f"M{n}", [P, NP_, CH]) for n in range(1, 6)]
        Tm = sb("Tm", [P, 4, CH, CH])
        shared = sb("shared", [P, 4 * B * (TB + 3)])
        pre = shared[:, :].rearrange("p (n b t) -> p n b t", n=4, b=B)
        kbd, qbd = [shared[:, 2 * n * B * P:2 * (n + 1) * B * P].rearrange("p (s b m) -> p s b m", s=2, b=B) for n in range(2)]
        usm = sb("usm", [P, 2, 4, B * DH])
        beta = hid[:, :, :].rearrange("p b d -> p (b d)").rearrange("p (g t) -> p g t", g=G)
        vsel3 = hid[:, :, :].rearrange("p b (n v) -> p (b n) v", v=DH)
        vsel = vsel3.rearrange("p (g b c) v -> p g b c v", g=G, b=B)
        vb = M5[:, :, :].rearrange("p (g b c) v -> p g b c v", g=G, b=B)
        obuf = M1[:, :, :].rearrange("p (g n) v -> p g n v", g=G)
        tbd, mbd, ktb = [qkv[:, 2 * n:2 * n + 2, :].rearrange("p r (b m) -> p r b m", b=B) for n in range(3)]
        m2b = qkv[:, 0:4, :].rearrange("p k t -> p (k t)")
        crs = sg[:, 0, :]

        xres = hT[:, :, :].rearrange("p k t -> p (k t)").rearrange("p (b d) -> p b d", b=B)
        xr = sb("xr", [P, B, D])
        cs = sb("cs", [P, 8, B * D])
        pkc = sb("pkc", [P, 3, NP_])
        rwt = sb("rwt", [P, 8, B, NE])
        idx = sb("idx", [P, B, 8], U32)

        def tokens(slot):
            return cs[:, slot, :].rearrange("p (b d) -> p b d", b=B)

        def channels(slot):
            return cs[:, slot, :].rearrange("p (k t) -> p k t", k=KC)

        n2, hx = tokens(0), tokens(0)
        n2T = x1T = channels(1)
        qx, dcv, combT = channels(2), channels(2), channels(2)
        prob = cs[:, 3, :].rearrange("p (h f n) -> p h f n", h=8, f=2)
        sT, hTT = channels(3), channels(3)
        probT = cs[:, 4, :].rearrange("p (h t) -> p h t", h=8)
        ax = cs[:, 5, :].rearrange("p (b h v) -> p b h v", b=B, h=H)
        at2 = cs[:, 6, :]
        ta = cs[:, 7, 0:256].rearrange("p (n v) -> p n v", v=DH)
        ye = cs[:, 4:6, :].rearrange("p s (r n) -> p (s r) n", r=2)
        comb = tokens(6)
        ot = tokens(6)
        gT = cs[0:HID, 7, 0:T]
        mx = pkc[:, 0, 0:16].rearrange("p (f h) -> p f h", f=2)
        rr = pkc[:, 1, 0:16]
        ars = pkc[:, 2, :]

        def flat(t3):
            return t3.rearrange("p a b -> p (a b)")

        bias_row = flat(cs[0:1, 0:4, :])[:, 0:NBIAS]
        bias_rest = flat(cs[0:1, 4:8, :])[:, 0:NBIAS]
        kbx_row = kbx[0:1, :, :, :].rearrange("p f b n -> p (f b n)")
        kq_row = kq[0:1, :, :, :, :, :].rearrange("p g b c x t -> p (g b c x t)")
        bias_part = [row[:, a:a + NBIAS // 2].bitcast(BF16) for row, a in ((kbx_row, 0), (kbx_row, NBIAS // 2), (kq_row, 0))]

        RAW = (0, 3, 1, 2)


        ld_w, ld_c, ld_b3, st_dbg = sem("ld_w"), sem("ld_c"), sem("ld_b3"), sem("st_dbg")
        vset, aset = sem("vset"), sem("aset")
        su = {n: sem("su_" + n) for n in ("trig_in", "trig", "split", "kproj", "vproj", "kv_sb", "exp_in", "exp_out", "ready", "tables")}
        x_in, xres_in, x_out = event("x_in", 16), event("xres_in", 16), event("x_out", 16)
        dchain, dchain2, achain, achain2 = sem("dchain"), sem("dchain2"), sem("achain"), sem("achain2")
        ev = {}
        for name, per in [("var1", 1), ("rstd1", 1), ("hid", 1), ("turn1_ps", 1), ("turn1_a", 1), ("turn1_v", 1),
                          ("rot_ps", 1), ("y", 1), ("y2_ps", 1), ("z", 1), ("zsq", 1), ("zsum_ps", 1), ("crs", 1), ("cond", 1),
                          ("proj_ps", 10), ("pre_sb", 10), ("bexp", 1), ("bone", 1), ("beta", 1), ("conv", 6), ("halo", 6), ("silu", 6), ("sq", 4), ("sum_ps", 4), ("rs", 4),
                          ("qk_norm", 4), ("db_ps", 1), ("db_sb", 1), ("db_exp", 1), ("db_one", 1), ("lg", 1), ("bt", 1), ("xpand", 2), ("lrep", 1),
                          ("gsum_ps", 1), ("gsel", 1), ("gexp", 1), ("grow_ps", 1), ("d_ready", 1), ("e_ready", 1), ("kbd", 32), ("qbd", 16), ("mbd", 16), ("tbd", 16),
                          ("raw_ps", 16), ("am", 4), ("tinv", 1), ("vb", 1), ("ks_ps", 16), ("r_ready", 16), ("kt_ps", 16), ("kt_sb", 16), ("u_ps", 16), ("u_sb", 16),
                          ("ds_ps", 16), ("s_new", 16), ("osq", 1), ("osum", 1), ("ors", 1), ("og", 1), ("wo_ps", 1), ("x1", 1),
                          ("var2", 2), ("rstd2", 2), ("normed", 3), ("turn_ps", 5), ("turn_a", 5), ("turn_v", 5),
                          ("qx_ps", 1), ("qx_sb", 1), ("sc_ps", 8), ("psub", 8), ("pexp", 8), ("pt_ps", 16), ("pt_sb", 16), ("pv_ps", 8), ("a_sb", 8),
                          ("asq", 1), ("asum", 1), ("ars", 1), ("wp_ps", 1), ("dconv", 1), ("pw_ps", 1), ("pws", 1), ("x1T", 1), ("lgt_ps", 1), ("top", 1), ("texp", 1),
                          ("moe_ps", 16), ("moe_act", 16), ("moe_acc", 16), ("mo_ps", 1), ("hrs", 1), ("hn", 1), ("ffd_ps", 1), ("gelu", 1), ("xh", 1),
                          ("ffu_ps", 1), ("done", 1)]:
            ev[name] = event(name, per)

        block = ctx.enter_context(nc.Block())

        def turns(eng, first, second):
            def take(*halves):
                for name, *args in ORDER:
                    for stages in halves:
                        if name in stages:
                            stages[name](*args)

            take(first(0))
            with eng.Fori(1, NI) as i:
                take(first(i), second(i - 1))
            take(second(NI - 1))

        @block.sync
        def _(sp):
            sp.dma_start(l_sb[:, :], cols[:, :]).then_inc(ld_c, 16)
            sp.dma_start(c_sb[:, :], consts[:, :]).then_inc(ld_c, 16)
            sp.dma_start(bias_row, biases[:, :]).then_inc(ld_c, 16)
            sp.dma_start(Tm[:, :, :, :].rearrange("p a b c -> p (a b c)"), teye[:, :]).then_inc(ld_c, 16)
            for (name, dst) in (("ramp", flat(qkv[:, 0:3, :])[:, 0:1056]), ("wk", flat(hT[:, 0:1, :])), ("wv", flat(hT[:, 1:2, :])),
                                ("ctx", flat(kn[:, 0:1, :])), ("ctxd", flat(xt[:, :, :]))):
                sp.dma_start(dst, scratch[:, SOFF[name][0]:SOFF[name][1]]).then_inc(ld_w, 16)
            sp.dma_start(w_sb[:, :], weights[:, :]).then_inc(ld_w, 16)
            sp.wait_ge(su["split"], 1)
            for n in range(3):
                sp.dma_start(bias3[n:n + 1, :], bias_part[n]).then_inc(ld_b3, 16)
            sp.wait_ge(su["ready"], 1)

            def rows(array, n):
                lo_ = n * TB
                return array[:, lo_:lo_ + TB, :] if isinstance(n, int) else array[:, bass.ds(lo_, TB), :]

            def load(dst, event_, n):
                sp.dma_start(dst[:, :, :], rows(x, n).rearrange("b p d -> p b d")).then_inc(event_.sem, 16)

            def store(n):
                sp.wait_ge(ev["done"].sem, n + 1)
                sp.dma_start(rows(out, n).rearrange("b p d -> p b d"), ot[:, :, :]).then_inc(x_out.sem, 16)

            def load_residual(i, earlier=True):
                if earlier:
                    sp.wait_ge(x_out.sem, (i - 1) * 16)
                sp.wait_ge(ev["proj_ps"].sem, ev["proj_ps"].at(i, 10))
                sp.wait_ge(ev["db_ps"].sem, ev["db_ps"].at(i))
                load(xres, xres_in, i)

            def turn(i, first=False, last=False):
                if not last:
                    sp.wait_ge(ev["hid"].sem, i + 1)
                    load(xt, x_in, i + 1)
                load_residual(i, not first)
                store(i - 1)

            load(xt, x_in, 0)
            sp.wait_ge(ev["hid"].sem, 1)
            load(xt, x_in, 1)
            load_residual(0, False)
            turn(1, first=True)
            with sp.Fori(2, NI - 1) as i:
                turn(i)
            turn(NI - 1, last=True)
            store(NI - 1)
            sp.wait_ge(x_out.sem, 16 * NI)

        @block.gpsimd
        def _(pool):
            tt = nc.gpsimd.tensor_tensor

            def first(i):
                def up(name, k=1):
                    pool.wait_ge(ev[name].sem, ev[name].at(i, k))

                def fin(name, ins):
                    ins.then_inc(ev[name].sem, 1)

                def bdiag(dst, src, name):
                    fin(name, tt(dst.rearrange("p b (h t) -> p b h t", h=HG), src.unsqueeze(2).to_broadcast([P, B, HG, CH]),
                                 bd.unsqueeze(1).unsqueeze(3).to_broadcast([P, B, HG, CH]), ALU.mult))

                kch = lambda g, c: kn[:, g, :].rearrange("p (b c t) -> p b c t", b=B, c=NC)[:, :, c, :]

                def spread():
                    up("lg")
                    up("bt")
                    for src, dst in ((lgc, rota), (btc, rotb)):
                        fin("xpand", tt(dst[:, :].rearrange("p (a c h) -> p a c h", a=B * G, c=NC),
                                        src[:, :, :].rearrange("p b (g h) -> p (b g) h", g=G).unsqueeze(2).to_broadcast([P, B * G, NC, HG]),
                                        C("mc").unsqueeze(1).unsqueeze(3).to_broadcast([P, B * G, NC, HG]), ALU.mult))
                    fin("lrep", nc.gpsimd.tensor_copy(M1[:, :, :], flat(lgc[:, :, :]).unsqueeze(2).to_broadcast([P, B * H, CH])))

                def raw(r):
                    for s in range(4 * r, 4 * r + 4):
                        if s == 0:
                            up("qk_norm", 4)
                        if s >= 2:
                            up("raw_ps", s - 1)
                        bdiag(kbd[:, s % 2, :, :], kch(s // NC, s % NC), "kbd")

                def old(s):
                    if s < 2:
                        up("raw_ps", 15 + s)
                    else:
                        up("kt_ps", s - 1)
                        up("ks_ps", s - 1)
                    bdiag(kbd[:, s % 2, :, :], kch(s % G, s // G), "kbd")
                    bdiag(qbd[:, s % 2, :, :], kq[:, s % G, :, s // G, 1, :], "qbd")

                def bd_(s):
                    if s >= 2:
                        up("ds_ps", s - 1)
                    elif s == 0:
                        up("am", 4)
                        up("vb")
                    bdiag(mbd[:, s % 2, :, :], M4[:, :, :].rearrange("p (b g c) t -> p b g c t", b=B, g=G)[:, :, s % G, s // G, :], "mbd")

                def onorm():
                    up("s_new", NSUB)
                    fin("osq", tt(flat(M2[:, :, :]), flat(M1[:, :, :]), flat(M1[:, :, :]), ALU.mult))

                return {"spread": spread, "raw": raw, "old": old, "bd": bd_, "onorm": onorm}

            def second(j):
                def up(name, k=1):
                    pool.wait_ge(ev[name].sem, ev[name].at(j, k))

                def anorm():
                    up("a_sb", 8)
                    if isinstance(j, int):
                        pool.wait_ge(x_out.sem, 16 * j)
                    else:
                        pool.wait_ge(xres_in.sem, xres_in.at(j + 1, 16))
                    a2 = ax.rearrange("p b h v -> p (b h v)")
                    tt(at2, a2, a2, ALU.mult).then_inc(ev["asq"].sem, 1)

                def ffn():
                    up("hn")
                    tt(flat(xr[:, :, :]), flat(xr[:, :, :]), flat(hx), ALU.add).then_inc(ev["xh"].sem, 1)

                return {"anorm": anorm, "ffn": ffn}

            turns(pool, first, second)

        @block.scalar
        def _(act):
            A = nc.scalar.activation
            act.wait_ge(su["trig_in"], 1)
            A(small[:, 16:18], small[:, 18:20], ACT.Sin).then_inc(su["trig"], 1)
            act.wait_ge(su["exp_in"], 1)
            act.wait_ge(ld_w, 16 * 6)
            A(flat(qkv[:, 0:3, :])[:, 0:1056], flat(qkv[:, 0:3, :])[:, 0:1056], ACT.Exp, scale=-1.0)
            A(small[:, 20:22], small[:, 22:24], ACT.Exp).then_inc(su["exp_out"], 1)
            act.wait_ge(su["kproj"], 1)
            for h2 in range(2):
                nc.scalar.copy(kn[:, 1, h2 * 256:h2 * 256 + 256], bank[h2][:, 0:256])
            act.wait_ge(su["vproj"], 1)
            for n in range(2):
                nc.scalar.copy(flat(M3[:, 32 * n:32 * n + 32, :]), bank[2 + n][:, :]).then_inc(su["kv_sb"], 1)

            def inv_sqrt(ch, dst, src, eps, scale, done):
                ch.do(A(dst, src, ACT.Ln, bias=eps, scale=scale))
                A(dst, dst, ACT.Exp, scale=-0.5).then_inc(ev[done].sem, 1)

            def log_exp_tables():
                nc.scalar.preload_act_table_set("natural_log_exp_and_others")

            def first(i):
                ch = Chain(act, achain, i, ACT_AB)

                def up(name, k=1):
                    act.wait_ge(ev[name].sem, ev[name].at(i, k))

                def fin(name, ins):
                    ins.then_inc(ev[name].sem, 1)

                def ln1():
                    log_exp_tables()
                    up("var1")
                    inv_sqrt(ch, rstd[:, 0, :], mv[:, 0, :, 1], eps5, 1.0, "rstd1")

                def turn1():
                    up("turn1_ps")
                    fin("turn1_a", nc.scalar.copy(hT[:, 0, :], bank[0][:, :]))

                def cond():
                    up("z")
                    fin("zsq", A(qkv[:, 1, :], qkv[:, 0, :], ACT.Square))
                    up("zsum_ps")
                    inv_sqrt(ch, crs, bank[1][:, :], eps6, 1.0 / P, "crs")

                def proj(j):
                    up("proj_ps", j + 1)
                    src = bank[j % 4][:, :]
                    if j < 2:
                        fin("pre_sb", A(beta[:, j, :], src, ACT.Exp, bias=negb[:, j:j + 1], scale=-1.0))
                    elif j < 8:
                        n = j - 2
                        if n >= 4:
                            up("halo", n - 3)
                        A(qkv[:, n, :], src, ACT.Identity, bias=bw3[:, n:n + 1], scale=L("conv", 4 * n + 3, 4 * n + 4))
                        fin("pre_sb", A(pre[:, n % 4, :, 3:TB + 3], src.rearrange("p (b t) -> p b t", b=B), ACT.Identity, bias=L("bproj", n, n + 1)))
                    else:
                        fin("pre_sb", A(sg[:, j - 8, :], src, ACT.Silu, bias=L("bproj", j - 2, j - 1)))

                def beta_():
                    up("bone")
                    ch.do(A(flat(beta), flat(beta), ACT.Ln))
                    fin("beta", A(flat(beta), flat(beta), ACT.Exp, scale=-1.0))

                def silu():
                    for n in range(6):
                        up("conv", n + 1)
                        fin("silu", A(qkv[:, n, :], qkv[:, n, :], ACT.Silu))
                    log_exp_tables()

                def sum_(j):
                    if j == 0:
                        up("silu", 6)
                        up("db_ps")
                    if j >= 2:
                        up("sum_ps", j - 1)
                    fin("sq", A((rota, rotb)[j % 2][:, :], qkv[:, j, :], ACT.Square))
                    up("sum_ps", j + 1)
                    if j >= 2:
                        up("qk_norm", j - 1)
                    inv_sqrt(ch, flat((M2, M4)[j % 2][:, :, :])[:, 0:512], bank[(3, 0)[j % 2]][:, :], eps6, 1.0, "rs")

                def spread():
                    up("db_sb")
                    fin("db_exp", A(edb[:, :, :], edb[:, :, :], ACT.Exp, scale=-1.0))
                    up("db_one")
                    fin("lg", A(lgc[:, :, :], edb[:, :, 0:H], ACT.Ln))

                def decay():
                    up("gsel")
                    A(eG, Gp, ACT.Exp)
                    A(eGC, GCp, ACT.Exp)
                    fin("gexp", A(eD, eD, ACT.Exp))

                def grow():
                    up("d_ready")
                    fin("e_ready", A(flat(M2[:, :, :]), flat(M2[:, :, :]), ACT.Exp))

                def old(s):
                    up("kt_ps", s + 1)
                    if s == 0:
                        up("vb")
                    if s >= 2:
                        up("ds_ps", s - 1)
                    fin("kt_sb", nc.scalar.copy(flat(ktb[:, s % 2, :, :]), bank[s % 2][:, :]))

                def onorm():
                    log_exp_tables()
                    up("osum")
                    inv_sqrt(ch, ors, ors, eps6, 1.0 / DH, "ors")
                    if isinstance(i, int):
                        assert ch.count == ACT_AB, ch.count

                return {"ln1": ln1, "turn1": turn1, "cond": cond, "proj": proj, "beta": beta_, "silu": silu, "sum": sum_, "spread": spread,
                        "decay": decay, "grow": grow, "old": old, "onorm": onorm}

            def second(j):
                ch = Chain(act, achain2, j, ACT_CD)

                def up(name, k=1):
                    act.wait_ge(ev[name].sem, ev[name].at(j, k))

                def fin(name, ins):
                    ins.then_inc(ev[name].sem, 1)

                def layer_rstd(k):
                    up("var2", k)
                    inv_sqrt(ch, rstd[:, 1, :], mv[:, 1, :, 1], eps5, 1.0, "rstd2")

                def turned(k, dst, r3=False):
                    up("turn_ps", k)
                    fin("turn_a", nc.scalar.copy(dst, bank[4][:, :].rearrange("p (b t) -> p b t", b=B) if r3 else bank[4][:, :]))

                def ln2():
                    log_exp_tables()
                    layer_rstd(1)

                def turn2():
                    turned(1, n2T[:, 0, :])
                    up("qx_ps")
                    nc.scalar.copy(qx[:, 0, :], bank[6][:, :])
                    fin("qx_sb", nc.scalar.copy(qx[:, 1, :], bank[7][:, :]))

                def max_(u):
                    up("psub", u + 1)
                    fin("pexp", A(cs[:, 3, :], cs[:, 3, :], ACT.Exp, scale=XSCALE))

                def pt(u):
                    for n in range(2):
                        up("pt_ps", 2 * u + n + 1)
                        if u and not n:
                            up("pv_ps", u)
                        fin("pt_sb", nc.scalar.copy(flat(probT[:, 4 * n:4 * n + 4, :]), bank[6][:, :]))

                def anorm():
                    up("asum")
                    inv_sqrt(ch, ars, ars, eps5, 1.0 / DH, "ars")
                    turned(2, n2T[:, 0, :])

                def ln3():
                    layer_rstd(2)

                def turn4():
                    turned(3, fT[:, 0, :, 2:TB + 2], r3=True)

                def pw_():
                    up("pw_ps")
                    A(sT[:, 0, :], bank[6][:, :], ACT.Silu, bias=L("pwb", 0, 1))
                    fin("pws", A(sT[:, 1, :], bank[7][:, :], ACT.Silu, bias=L("pwb", 1, 2)))

                def top():
                    up("top")
                    fin("texp", A(rwt[:, 3, :, 1], rwt[:, 3, :, 0], ACT.Exp))

                def moe(u):
                    up("moe_ps", u + 1)
                    if u >= 4:
                        up("moe_acc", u - 3)
                    fin("moe_act", A(ye[:, u % 4, :], bank[4 + (u + 1) % 4][:, :], ACT.Silu))

                def turn5():
                    turned(4, combT[:, 0, :])

                def hnorm():
                    up("mo_ps")
                    for n in range(2):
                        last = nc.scalar.copy(flat(hx[:, 2 * n:2 * n + 2, :]), bank[6 + n][:, :])
                    ch.do(last)
                    for b in range(B):
                        last = A(ye[:, b, 0:D], hx[:, b, :], ACT.Square, accum_out=rstd[:, 1, b:b + 1])
                    ch.do(last)
                    inv_sqrt(ch, rstd[:, 1, :], rstd[:, 1, :], eps6, 1.0 / D, "hrs")

                def ffn():
                    turned(5, hTT[:, 0, :])
                    up("ffd_ps")
                    fin("gelu", A(gT, bank[6][0:HID, :], ACT.Gelu, bias=L("fdb")[0:HID, :]))
                    if isinstance(j, int):
                        assert ch.count == ACT_CD, ch.count

                return {"ln2": ln2, "turn2": turn2, "max": max_, "pt": pt, "anorm": anorm, "ln3": ln3, "turn4": turn4, "pw": pw_, "top": top,
                        "moe": moe, "turn5": turn5, "hnorm": hnorm, "ffn": ffn}

            turns(act, first, second)

        @block.vector
        def _(dve):
            V = nc.vector
            tt, ts, stt, red = V.tensor_tensor, V.tensor_scalar, V.scalar_tensor_tensor, V.tensor_reduce
            do = Chain(dve, vset).do

            dve.wait_ge(ld_c, 16 * 4)
            do(V.memset(eps5, 1e-5))
            do(V.memset(eps6, 1e-6))
            turns_, r = small[:, 24:25], small[:, 18:19]
            magic = 1.5 * 2 ** 23
            do(ts(turns_, L("theta"), 0.15915494309189535, None, ALU.mult))
            do(ts(turns_, turns_, magic, None, ALU.add))
            do(ts(turns_, turns_, -magic, None, ALU.add))
            do(stt(r, turns_, -6.28125, L("theta"), ALU.mult, ALU.add))
            do(stt(r, turns_, -0.0019353071795864769, r, ALU.mult, ALU.add))
            do(ts(r, r, -3.1415925, 3.1415925, ALU.max, ALU.min))
            do(ts(small[:, 25:26], r, -1.0, None, ALU.mult))
            do(tt(small[:, 25:26], small[:, 25:26], r, ALU.max))
            do(ts(small[:, 19:20], small[:, 25:26], -1.0, 1.5707963267948966, ALU.mult, ALU.add))
            do(tt(small[:, 44:52], L("lam", 0, 8), L("lam", 8, 16), ALU.mult))
            do(tt(small[:, 52:60], L("lam", 16, 24), L("lam", 24, 32), ALU.mult))
            do(red(small[:, 22:24], small[:, 44:60].rearrange("p (a n) -> p a n", a=2), AX.X, ALU.add))
            V.nop().then_inc(su["trig_in"], 1)
            V.nop().then_inc(su["exp_in"], 1)
            do(ts(negb, L("bproj", 8, 10), -1.0, None, ALU.mult))
            do(tt(bw3, L("bproj", 0, 6), L("conv").rearrange("p (n t) -> p n t", t=4)[:, :, 3], ALU.mult))
            hi, mid, lo = bias_part
            do(V.tensor_copy(hi, bias_row))
            do(tt(bias_rest, bias_row, hi, ALU.subtract))
            do(V.tensor_copy(mid, bias_rest))
            do(tt(bias_rest, bias_rest, mid, ALU.subtract))
            do(V.tensor_copy(lo, bias_rest))
            V.nop().then_inc(su["split"], 1)
            for t_, value in ((ones3[:, :], 1.0), (zc[:, :], 0.0), (state[:, :, :, :], 0.0), (fT[:, :, :, 0:2], 0.0), (halo[:, :, :, :], 0.0)):
                do(V.memset(t_, value))
            dve.wait_ge(su["trig"], 1)
            do(V.tensor_copy(sinT[:, 0:1], small[:, 16:17]))
            do(V.tensor_copy(cosT[:, 0:1], small[:, 17:18]))
            n = 1
            while n < TB:
                do(ts(turns_, sinT[:, n - 1:n], -1.0, None, ALU.mult))
                do(ts(rota[:, 0:n], cosT[:, 0:n], cosT[:, n - 1:n], None, ALU.mult))
                do(ts(rotb[:, 0:n], sinT[:, 0:n], cosT[:, n - 1:n], None, ALU.mult))
                do(stt(cosT[:, n:2 * n], sinT[:, 0:n], turns_, rota[:, 0:n], ALU.mult, ALU.add))
                do(stt(sinT[:, n:2 * n], cosT[:, 0:n], sinT[:, n - 1:n], rotb[:, 0:n], ALU.mult, ALU.add))
                n *= 2
            do(ts(sinT[:, :], sinT[:, :], C("sgn"), None, ALU.mult))
            dve.wait_ge(su["exp_out"], 1)
            do(tt(turns_, small[:, 20:21], small[:, 21:22], ALU.subtract))
            do(ts(nlam, turns_, -1.0, -LAMBDA_INIT, ALU.mult, ALU.add))
            ramp = flat(qkv[:, 0:3, :])[:, 0:1056]
            do(ts(ramp, ramp, 1.0, None, ALU.add))
            do(V.reciprocal(ramp, ramp))
            do(stt(dw, dw, L("condnorm"), ramp, ALU.mult, ALU.mult))
            do(ts(W("wo"), W("wo"), L("outnorm"), None, ALU.mult))
            do(ts(W("wp"), W("wp"), L("subln"), 1.0 - LAMBDA_INIT, ALU.mult, ALU.mult))
            dve.wait_ge(su["kv_sb"], 2)
            vxv = vx[:, :, :, :].rearrange("p b h n -> p (b h) n")
            for f in range(2):
                do(ts(vxv[:, :, 17 * f:17 * f + 16], M3[:, :, :], C("half")[:, f:f + 1], None, ALU.mult))
                do(V.tensor_copy(vxv[:, :, 17 * f + 16], C("half")[:, f:f + 1].to_broadcast([P, B * H])))
            dve.wait_ge(ld_b3, 48)
            for h2 in range(2):
                for b in range(B):
                    do(tt(kbx[:, h2, b, :].rearrange("p (h n) -> p h n", h=8),
                          kn[:, 1, h2 * 256 + b * NK:h2 * 256 + b * NK + NK].unsqueeze(1).to_broadcast([P, 8, NK]),
                          C("hh").unsqueeze(2).to_broadcast([P, 8, NK]), ALU.mult))
            V.nop().then_inc(su["ready"], 1)

            def bc(ap, n):
                return ap.unsqueeze(2).to_broadcast([P, ap.shape[1], n])

            def landed():
                V.memset(spare, 0.0)

            r3 = lambda ap: ap.rearrange("p (b t) -> p b t", b=B)
            v3 = lambda ap: ap.rearrange("p (n t) -> p n t", t=CH)
            pv = lambda ap: ap.rearrange("p (b g c) -> p b g c", b=B, g=G)
            packs = lambda t: t[:, :, :].rearrange("p (b g c) t -> p b g c t", b=B, g=G)

            def statistics(ch, src, half, done):
                for b in range(B):
                    last = V.bn_stats(stat[:, half, b, :], src[:, b, :])
                ch.do(last)
                landed()
                for b in range(B):
                    last = V.bn_aggr(mv[:, half, b, :], stat[:, half, b, :])
                last.then_inc(ev[done].sem, 1)

            def normalise(src, dst, half, done):
                for b in range(B):
                    last = ts(dst[:, b, :], src[:, b, :], mv[:, half, b, 0:1], rstd[:, half, b:b + 1], ALU.subtract, ALU.mult)
                last.then_inc(ev[done].sem, 1)

            def first(i):
                ch = Chain(dve, dchain, i, DVE_AB)
                own, link = ch.do, ch.link

                def up(name, k=1):
                    dve.wait_ge(ev[name].sem, ev[name].at(i, k))

                def fin(name, ins):
                    ins.then_inc(ev[name].sem, 1)

                def ln1():
                    dve.wait_ge(x_in.sem, x_in.at(i, 16))
                    statistics(ch, xt, 0, "var1")
                    up("rstd1")
                    normalise(xt, hid, 0, "hid")

                def turn1():
                    up("turn1_ps")
                    fin("turn1_v", V.tensor_copy(hT[:, 1, :], bank[1][:, :]))

                cosb = cosT[:, :].unsqueeze(1).to_broadcast([P, B, TB])
                sinb = sinT[:, :].unsqueeze(1).to_broadcast([P, B, TB])

                def rot():
                    up("rot_ps")
                    tt(r3(rota[:, :]), r3(bank[2][:, :]), cosb, ALU.mult)
                    own(tt(r3(rotb[:, :]), r3(bank[3][:, :]), sinb, ALU.mult))
                    for b in range(B):
                        lo_, hi_ = b * TB, b * TB + TB
                        last = V.tensor_tensor_scan(qkv[:, 2, lo_:hi_], rota[:, lo_:hi_], rotb[:, lo_:hi_], zc[:, b:b + 1], ALU.add, ALU.add)
                    fin("y", last)

                def unrot():
                    up("y")
                    tt(r3(rota[:, :]), r3(qkv[:, 2, :]), cosb, ALU.mult)
                    up("y2_ps")
                    own(tt(r3(rotb[:, :]), r3(bank[0][:, :]), sinb, ALU.mult))
                    fin("z", tt(qkv[:, 0, :], rota[:, :], rotb[:, :], ALU.subtract))
                    up("z")
                    own(V.tensor_copy(zc[:, :], r3(qkv[:, 0, :])[:, :, TB - 1]))

                def cond():
                    up("crs")
                    fin("cond", tt(rotb[:, :], qkv[:, 0, :], crs, ALU.mult))

                def beta_():
                    up("pre_sb", 2)
                    fin("bone", ts(flat(beta), flat(beta), 1e19, 1.0, ALU.min, ALU.add))

                def conv(m):
                    pair = (2 * m, 2 * m + 1)
                    up("pre_sb", 2 * m + 4)
                    step = [0, 0]
                    for a, n in enumerate(pair):
                        step[a] = link(V.tensor_copy(pre[:, n % 4, :, 0:3], halo[:, n, :, :]))
                    for t in range(3):
                        for a, n in enumerate(pair):
                            ch.wait(step[a])
                            dst = r3(qkv[:, n, :])
                            ins = stt(dst, pre[:, n % 4, :, t:TB + t], L("conv", 4 * n + t, 4 * n + t + 1), dst, ALU.mult, ALU.add)
                            if t < 2:
                                step[a] = link(ins)
                            else:
                                fin("conv", ins)
                    for a, n in enumerate(pair):
                        fin("halo", V.tensor_copy(halo[:, n, :, :], pre[:, n % 4, :, TB:TB + 3]))

                def db():
                    up("db_ps")
                    d2 = bank[2][:, 0:B * 32].rearrange("p (b n) -> p b n", b=B)
                    ts(edb[:, :, 0:H], d2[:, :, 0:H], -43.0, None, ALU.max)
                    fin("db_sb", ts(edb[:, :, H:32], d2[:, :, H:32], -80.0, None, ALU.max))

                def sum_(j):
                    kqf = kq[:, :, :, :, :, :].rearrange("p g b c x t -> p g (b c) x t")
                    if j == 0:
                        up("silu", 6)
                        up("beta")
                    up("rs", j + 1)
                    tmp = (M2, M4)[j % 2][:, 0:32, :]
                    if j < 2:
                        fin("qk_norm", tt(kqf[:, j, :, 1, :], v3(qkv[:, j, :]), tmp, ALU.mult))
                    else:
                        own(tt(v3(kn[:, j - 2, :]), v3(qkv[:, j, :]), tmp, ALU.mult))
                        fin("qk_norm", tt(kqf[:, j - 2, :, 0, :], v3(kn[:, j - 2, :]), v3(beta[:, j - 2, :]), ALU.mult))

                def spread():
                    up("db_exp")
                    fin("db_one", ts(edb[:, :, :], edb[:, :, :], 1.0, None, ALU.add))
                    up("db_one")
                    fin("bt", V.reciprocal(btc[:, :, :], edb[:, :, H:32]))

                def half_select(dst, step):
                    m2w = m2b.rearrange("p (n w) -> p n w", w=32)
                    ch.wait(step)
                    own(ts(dst, m2w[:, :, 0:16], C("dup")[:, 0:1], None, ALU.mult))
                    own(stt(dst, m2w[:, :, 16:32], C("dup")[:, 1:2], dst, ALU.mult, ALU.add))

                def decay():
                    up("gsum_ps")
                    step = []
                    for n in range(3):
                        t8 = flat(((M3, M3, M5)[n])[:, 32 * (n % 2):32 * (n % 2) + 32, :]).rearrange("p (n h) -> p n h", h=HG)
                        step.append((t8, link(tt(t8, bank[1 + n][:, :].rearrange("p (n h) -> p n h", h=HG), bd.unsqueeze(1).to_broadcast([P, NP_, HG]), ALU.mult))))
                    for (t8, st_), dst in zip(step, (Gp, GCp, Bp)):
                        ch.wait(st_)
                        last = link(red(dst, t8, AX.X, ALU.add))
                    ch.wait()
                    fin("gsel", tt(eD, GCp, Gp, ALU.subtract))

                def grow():
                    up("grow_ps")
                    for n in range(2):
                        last = tt(M2[:, 32 * n:32 * n + 32, :], bank[1 + n][:, :].rearrange("p (n t) -> p n t", t=CH),
                                  bc(Gp[:, 32 * n:32 * n + 32], CH), ALU.subtract)
                    own(last)
                    fin("d_ready", stt(M2[:, :, :], M2[:, :, :], 0.0, C("neg").unsqueeze(1).to_broadcast([P, NP_, CH]), ALU.min, ALU.add))
                    up("gexp")
                    own(tt(bG, Bp, eG, ALU.mult))

                def am():
                    up("e_ready")
                    for r in range(4):
                        up("raw_ps", 4 * r + 4)
                        g, c0 = r // 2, (r % 2) * 4
                        raw = bank[RAW[r]][:, :].rearrange("p (c b x t) -> p c b x t", c=4, b=B, x=2)
                        e4, a4, m4 = [packs(t)[:, :, g, c0:c0 + 4, :].rearrange("p b c t -> p c b t") for t in (M2, M3, M4)]
                        tt(a4, raw[:, :, :, 0, :], e4, ALU.mult)
                        fin("am", tt(m4, raw[:, :, :, 1, :], e4, ALU.mult))

                prod = flat(M1[:, :, :])
                apr = M5[:, :, :].rearrange("p (h t) s -> p h t s", h=4)

                def solve(q):
                    if q == 0:
                        up("am", 4)
                        for ph in range(2):
                            last = V.transpose(apr[:, 2 * ph:2 * ph + 2, :, :].rearrange("p h t s -> p t h s"),
                                               M3[:, 32 * ph:32 * ph + 32, :].rearrange("p k t -> p t k"))
                        own(last)
                    for t in ((1, 2, 3, 4, 5, 6), (7, 8, 9, 10), (11, 12, 13), (14, 15))[q]:
                        pt_ = prod[:, 0:4 * t * t].rearrange("p (h j s) -> p h j s", h=4, j=t)
                        own(tt(pt_, Tm[:, :, 0:t, 0:t], apr[:, :, t, 0:t].unsqueeze(2).to_broadcast([P, 4, t, t]), ALU.mult))
                        own(red(Tm[:, :, 0:t, t], pt_, AX.X, ALU.add, negate=True))
                    if q == 3:
                        for ph in range(2):
                            last = V.transpose(M3[:, 32 * ph:32 * ph + 32, :].rearrange("p k t -> p t k"),
                                               Tm[:, 2 * ph:2 * ph + 2, :, :].rearrange("p h j t -> p t (h j)"))
                        fin("tinv", last)
                        for g in range(G):
                            last = tt(vb[:, g, :, :, :], vsel[:, g, :, :, :], pv(Bp)[:, :, g, :].unsqueeze(3).to_broadcast([P, B, NC, DH]), ALU.mult)
                        fin("vb", last)

                def vpack():
                    for g in range(G):
                        last = V.transpose(m2b[:, g * 1024:g * 1024 + 1024], v3(qkv[:, 4 + g, :]).unsqueeze(2).to_broadcast([P, 32, 2, CH]))
                    half_select(vsel3, link(last))

                def bd_(s):
                    if s == 0:
                        up("tinv")
                        up("vb")
                    if s >= 2:
                        up("u_ps", s - 1)
                    fin("tbd", tt(tbd[:, s % 2, :, :].rearrange("p b (h t) -> p b h t", h=HG),
                                  packs(M3)[:, :, s % G, s // G, :].unsqueeze(2).to_broadcast([P, B, HG, CH]),
                                  bd.unsqueeze(1).unsqueeze(3).to_broadcast([P, B, HG, CH]), ALU.mult))

                def chunk(s):
                    c, g, X = s // G, s % G, bank[2 + s % 2]
                    xv = lambda n: X[:, 64 * n:64 * n + 64].rearrange("p (b v) -> p b v", b=B)
                    sm = lambda n: usm[:, s % 2, n, :].rearrange("p (b v) -> p b v", b=B)
                    col = lambda ap: pv(ap)[:, :, g, c].unsqueeze(2).to_broadcast([P, B, DH])
                    return c, g, xv, sm, col

                def old(s):
                    c, g, xv, sm, col = chunk(s)
                    up("ks_ps", s + 1)
                    step = link(tt(sm(0), xv(0), col(bG), ALU.mult))
                    tt(sm(3), xv(1), col(eG), ALU.mult)
                    ch.wait(step)
                    fin("r_ready", tt(sm(0), vb[:, g, :, c, :], sm(0), ALU.subtract))
                    link(tt(state[:, :, g, :], state[:, :, g, :], col(eGC), ALU.mult))

                def u_(s):
                    c, g, xv, sm, col = chunk(s)
                    up("u_ps", s + 1)
                    V.tensor_copy(sm(1), xv(2))
                    fin("u_sb", tt(sm(2), xv(2), col(eD), ALU.mult))

                def new(s):
                    c, g, xv, sm, col = chunk(s)
                    up("ds_ps", s + 1)
                    ch.wait()
                    tt(state[:, :, g, :], state[:, :, g, :], xv(3), ALU.add)
                    fin("s_new", tt(obuf[:, g, :, :].rearrange("p (b c) v -> p b c v", b=B)[:, :, c, :], xv(4), sm(3), ALU.add))

                def onorm():
                    up("osq")
                    fin("osum", red(ors, M2[:, :, :], AX.X, ALU.add))
                    up("ors")
                    own(tt(M1[:, :, :], M1[:, :, :], bc(ors, DH), ALU.mult))
                    for g in range(G):
                        last = V.transpose(m2b[:, g * 1024:g * 1024 + 1024], obuf[:, g, :, :].unsqueeze(2).to_broadcast([P, 32, 2, DH]))
                    half_select(v3(flat(kn[:, :, :])), link(last))
                    fin("og", tt(flat(kn[:, :, :]), flat(kn[:, :, :]), flat(sg[:, :, :]), ALU.mult))

                def x1_():
                    up("wo_ps")
                    dve.wait_ge(xres_in.sem, xres_in.at(i, 16))
                    if not (isinstance(i, int) and i == 0):
                        dve.wait_ge(ev["done"].sem, ev["done"].at(i - 1))
                    for n in range(2):
                        last = tt(flat(xr[:, 2 * n:2 * n + 2, :]), bank[n][:, :], flat(xres[:, 2 * n:2 * n + 2, :]), ALU.add)
                    fin("x1", last)
                    if isinstance(i, int):
                        assert ch.count == DVE_AB, ch.count

                return {"ln1": ln1, "turn1": turn1, "rot": rot, "unrot": unrot, "cond": cond, "beta": beta_, "conv": conv, "db": db, "sum": sum_,
                        "spread": spread, "decay": decay, "grow": grow, "am": am, "solve": solve, "vpack": vpack, "bd": bd_, "old": old, "u": u_,
                        "new": new, "onorm": onorm, "x1": x1_}

            def second(j):
                ch = Chain(dve, dchain2, j, DVE_CD)
                own, link = ch.do, ch.link

                def up(name, k=1):
                    dve.wait_ge(ev[name].sem, ev[name].at(j, k))

                def fin(name, ins):
                    ins.then_inc(ev[name].sem, 1)

                def layer_norm(k, done):
                    statistics(ch, xr, 1, "var2")
                    up("rstd2", k)
                    normalise(xr, n2, 1, "normed")

                def turned(k, dst, src=None):
                    up("turn_ps", k)
                    fin("turn_v", V.tensor_copy(dst, bank[5][:, :] if src is None else src))

                def ln2():
                    up("x1")
                    layer_norm(1, 1)

                def turn2():
                    turned(1, n2T[:, 1, :])

                def max_(u):
                    up("sc_ps", u + 1)
                    sc = [bank[4 + f][:, :].rearrange("p (h n) -> p h n", h=8) for f in range(2)]
                    step = [link(red(mx[:, f, :], sc[f], AX.X, ALU.max)) for f in range(2)]
                    if u:
                        up("pt_ps", 2 * u)
                    for f in range(2):
                        ch.wait(step[f])
                        last = tt(prob[:, :, f, :], sc[f], bc(mx[:, f, :], NK), ALU.subtract)
                    fin("psub", last)

                def av(u):
                    b, hc = u // 2, u % 2
                    up("pv_ps", u + 1)
                    ov = bank[7][:, 0:272].rearrange("p (n v) -> p n v", v=17)
                    own(V.reciprocal(rr, ov[:, :, 16]))
                    r2 = rr.rearrange("p (h f) -> p h f", f=2)
                    own(ts(r2[:, :, 1], r2[:, :, 1], nlam, None, ALU.mult))
                    own(tt(ta, ov[:, :, 0:16], bc(rr, DH), ALU.mult))
                    tav = ta.rearrange("p (h f) v -> p h f v", f=2)
                    fin("a_sb", tt(ax[:, b, 8 * hc:8 * hc + 8, :], tav[:, :, 0, :], tav[:, :, 1, :], ALU.add))

                def anorm():
                    up("asq")
                    fin("asum", red(ars, at2.rearrange("p (n v) -> p n v", v=DH), AX.X, ALU.add))
                    up("ars")
                    ax3 = ax.rearrange("p b h v -> p (b h) v")
                    fin("normed", tt(ax3, ax3, bc(ars, DH), ALU.mult))
                    turned(2, n2T[:, 1, :])

                def wp_():
                    up("wp_ps")
                    for n in range(2):
                        x_ = flat(xr[:, 2 * n:2 * n + 2, :])
                        last = tt(x_, bank[6 + n][:, :], x_, ALU.add)
                    own(last)

                def ln3():
                    layer_norm(2, 3)

                def turn4():
                    turned(3, fT[:, 1, :, 2:TB + 2], r3(bank[5][:, :]))

                def dconv():
                    up("turn_v", 3)
                    up("turn_a", 3)
                    step = []
                    for k in range(KC):
                        step.append(link(ts(r3(dcv[:, k, :]), fT[:, k, :, 0:TB], L("dwk", 3 * k, 3 * k + 1), L("dwb", k, k + 1), ALU.mult, ALU.add)))
                    for t in (1, 2):
                        for k in range(KC):
                            dst = r3(dcv[:, k, :])
                            ch.wait(step[k])
                            last = stt(dst, fT[:, k, :, t:TB + t], L("dwk", 3 * k + t, 3 * k + t + 1), dst, ALU.mult, ALU.add)
                            if t == 1:
                                step[k] = link(last)
                    fin("dconv", last)
                    V.tensor_copy(fT[:, :, :, 0:2], fT[:, :, :, TB:TB + 2])

                def pw_():
                    up("pws")
                    for k in range(KC):
                        last = tt(r3(x1T[:, k, :]), r3(sT[:, k, :]), fT[:, k, :, 2:TB + 2], ALU.add)
                    fin("x1T", last)

                def top():
                    up("lgt_ps")
                    own(V.tensor_copy(rwt[:, 0, :, :], bank[4][:, 0:32].rearrange("p (b e) -> p b e", b=B)))
                    landed()
                    for b in range(B):
                        last = V.max(rwt[:, 1, b, :], rwt[:, 0, b, :])
                    own(last)
                    fin("top", tt(rwt[:, 3, :, 0], rwt[:, 1, :, 1], rwt[:, 1, :, 0], ALU.subtract))
                    for b in range(B):
                        last = V.max_index(idx[:, b, :], rwt[:, 1, b, :], rwt[:, 0, b, :])
                    own(last)
                    own(V.tensor_copy(rwt[:, 2, :, :], idx[:, :, :]))
                    for n in range(2):
                        link(tt(rwt[:, 4 + n, :, :], C("iota").unsqueeze(1).to_broadcast([P, B, NE]), bc(rwt[:, 2, :, n], NE), ALU.is_equal))
                    up("texp")
                    own(ts(rwt[:, 3, :, 2], rwt[:, 3, :, 1], 1.0, None, ALU.add))
                    own(V.reciprocal(rwt[:, 3, :, 3], rwt[:, 3, :, 2]))
                    own(tt(rwt[:, 3, :, 4], rwt[:, 3, :, 1], rwt[:, 3, :, 3], ALU.mult))
                    for n in range(2):
                        last = tt(rwt[:, 4 + n, :, :], rwt[:, 4 + n, :, :], bc(rwt[:, 3, :, 3 + n], NE), ALU.mult)
                    own(last)
                    own(tt(rwt[:, 6, :, :], rwt[:, 4, :, :], rwt[:, 5, :, :], ALU.add))

                def acc(u):
                    b, ep = u // 4, u % 4
                    up("moe_act", u + 1)
                    for e2 in range(2):
                        e = 2 * ep + e2
                        src, wgt = ye[:, u % 4, e2 * D:e2 * D + D], rwt[:, 6, b, e:e + 1]
                        if e == 0:
                            ins = ts(comb[:, b, :], src, wgt, None, ALU.mult)
                        else:
                            if not e2:
                                up("moe_acc", u)
                            ins = stt(comb[:, b, :], src, wgt, comb[:, b, :], ALU.mult, ALU.add)
                        if e2:
                            fin("moe_acc", ins)
                        else:
                            own(ins)

                def turn5():
                    turned(4, combT[:, 1, :])

                def hnorm():
                    up("hrs")
                    for b in range(B):
                        last = stt(hx[:, b, :], hx[:, b, :], rstd[:, 1, b:b + 1], W("normw"), ALU.mult, ALU.mult)
                    fin("hn", last)

                def ffn():
                    turned(5, hTT[:, 1, :])
                    up("xh")
                    up("ffu_ps")
                    for n in range(2):
                        last = tt(flat(ot[:, 2 * n:2 * n + 2, :]), bank[4 + n][:, :], flat(xr[:, 2 * n:2 * n + 2, :]), ALU.add)
                    fin("done", last)
                    if isinstance(j, int):
                        assert ch.count == DVE_CD, ch.count

                return {"ln2": ln2, "turn2": turn2, "max": max_, "av": av, "anorm": anorm, "wp": wp_, "ln3": ln3, "turn4": turn4, "dconv": dconv,
                        "pw": pw_, "top": top, "acc": acc, "turn5": turn5, "hnorm": hnorm, "ffn": ffn}

            turns(dve, first, second)

        @block.tensor
        def _(pe):
            mm = nc.tensor.matmul

            def over_k(dst, lhs, rhs, n=KC):
                for k in range(n):
                    last = mm(dst, lhs(k), rhs(k), start=k == 0, stop=k == n - 1)
                return last

            def bias(dst, name, a=0, b=None):
                lo_, hi_ = BOFF[name]
                return mm(dst, ones3[:, :], bias3[:, lo_ + a:(hi_ if b is None else lo_ + b)], start=False, stop=True)

            def transposes(src, at):
                for k in range(KC):
                    for b in range(B):
                        last = nc.tensor.transpose(bank[at + k][:, b * TB:b * TB + TB], src[:, b, k * P:k * P + P], ident)
                return last

            def to_tokens(at, lhs, rhs, name):
                for b in range(B):
                    dst = bank[at + b // 2][:, (b % 2) * D:(b % 2) * D + D]
                    for k in range(KC):
                        mm(dst, lhs[:, k, b * TB:b * TB + TB], rhs[:, k, :], start=k == 0, stop=False)
                    last = bias(dst, name)
                return last

            pe.wait_ge(ld_w, 16 * 6)
            wk_, wv_ = [hT[:, n, :].rearrange("p (k n) -> p k n", k=KC) for n in range(2)]
            ctx_ = kn[:, 0, :].rearrange("p (k n) -> p k n", k=KC)
            ctxd_ = flat(xt[:, :, :]).rearrange("p (k b n) -> p k b n", k=KC, b=B)
            for h2 in range(2):
                last = over_k(bank[h2][:, 0:256], lambda k: wk_[:, k, h2 * P:h2 * P + P], lambda k: ctx_[:, k, :])
            last.then_inc(su["kproj"], 1)
            for b in range(B):
                last = over_k(bank[2 + b // 2][:, (b % 2) * D:(b % 2) * D + D], lambda k: ctxd_[:, k, b, :], lambda k: wv_[:, k, :])
            last.then_inc(su["vproj"], 1)
            pe.wait_ge(su["ready"], 1)

            def first(i):
                def up(name, k=1):
                    pe.wait_ge(ev[name].sem, ev[name].at(i, k))

                def fin(name, ins):
                    ins.then_inc(ev[name].sem, 1)

                def turn1():
                    up("hid")
                    fin("turn1_ps", transposes(hid, 0))

                def rot():
                    up("turn1_a")
                    up("turn1_v")
                    for n in range(2):
                        last = over_k(bank[2 + n][:, :], lambda k: cin[:, k, n * P:n * P + P], lambda k: hT[:, k, :])
                    fin("rot_ps", last)

                def unrot():
                    up("y")
                    fin("y2_ps", mm(bank[0][:, :], C("swap"), qkv[:, 2, :], start=True, stop=True))

                def cond():
                    up("zsq")
                    fin("zsum_ps", mm(bank[1][:, :], C("ones"), qkv[:, 1, :], start=True, stop=True))

                def proj(j):
                    if j == 0:
                        up("cond")
                    if j >= 4:
                        up("pre_sb", j - 3)
                    cc = 1024 + j * P if j < 2 else (j - 2) * P
                    dst = bank[j % 4][:, :]
                    for k in range(KC):
                        last = mm(dst, ctrl[:, k, cc:cc + P], hT[:, k, :], start=k == 0, stop=j >= 8 and k == 1)
                    if j < 8:
                        dc = 768 + j * P if j < 2 else (j - 2) * P
                        last = mm(dst, dw[:, dc:dc + P], rotb[:, :], start=False, stop=True)
                    fin("proj_ps", last)

                def db():
                    up("pre_sb", 7)
                    for b in range(B):
                        dst = bank[2][:, b * 32:b * 32 + 32]
                        for k in range(KC):
                            mm(dst, hT[:, k, b * TB:b * TB + TB], ctrl[:, k, 1280:1312], start=k == 0, stop=False)
                        mm(dst, rotb[:, b * TB:b * TB + TB], dw[:, 1024:1056], start=False, stop=False)
                        last = bias(dst, "db")
                    fin("db_ps", last)

                def sum_(j):
                    up("sq", j + 1)
                    if j == 0:
                        up("pre_sb", 10)
                    if j >= 2:
                        up("rs", j - 1)
                    fin("sum_ps", mm(bank[(3, 0)[j % 2]][:, :], C("bones"), (rota, rotb)[j % 2][:, :], start=True, stop=True))

                def decay():
                    up("xpand", 2)
                    up("rs", 4)
                    mm(bank[1][:, :], C("tri"), rota[:, :], start=True, stop=True)
                    mm(bank[2][:, :], C("negones"), rota[:, :], start=True, stop=True)
                    fin("gsum_ps", mm(bank[3][:, :], C("delta"), rotb[:, :], start=True, stop=True))

                def grow():
                    up("gsel")
                    up("lrep")
                    lrep = flat(M1[:, :, :])
                    for n in range(B * G):
                        last = mm(bank[1 + n // 4][:, (n % 4) * P:(n % 4) * P + P], lrep[:, n * P:n * P + P], C("triblk"), start=True, stop=True)
                    fin("grow_ps", last)

                def raw(r):
                    if r == 0:
                        up("rs", 4)
                    elif r == 2:
                        up("d_ready")
                    for s in range(4 * r, 4 * r + 4):
                        g, c = s // NC, s % NC
                        up("kbd", s + 1)
                        for b in range(B):
                            at = (s % 4) * P + b * 2 * CH
                            last = mm(bank[RAW[r]][:, at:at + 2 * CH], kbd[:, s % 2, b, :],
                                      kq[:, g, b, c, :, :].rearrange("p x t -> p (x t)"), start=True, stop=True)
                        fin("raw_ps", last)

                def old(s):
                    g, X = s % G, bank[2 + s % 2]
                    up("kbd", NSUB + s + 1)
                    up("qbd", s + 1)
                    if s == 0:
                        up("am", 4)
                    if s >= 2:
                        up("kt_sb", s - 1)
                    for b in range(B):
                        last = nc.tensor.transpose(bank[s % 2][:, b * P:b * P + P], kbd[:, s % 2, b, :], ident)
                    fin("kt_ps", last)
                    if s >= 2:
                        up("s_new", s - 1)
                    for n, src in enumerate((kbd, qbd)):
                        for b in range(B):
                            last = mm(X[:, 64 * n + DH * b:64 * n + DH * b + DH], src[:, s % 2, b, :], state[:, b, g, :], start=True, stop=True)
                    fin("ks_ps", last)

                def u_(s):
                    X = bank[2 + s % 2]
                    up("tbd", s + 1)
                    up("r_ready", s + 1)
                    for b in range(B):
                        last = mm(X[:, 128 + DH * b:128 + DH * b + DH], tbd[:, s % 2, b, :], usm[:, s % 2, 0, DH * b:DH * b + DH], start=True, stop=True)
                    fin("u_ps", last)

                def new(s):
                    X = bank[2 + s % 2]
                    up("mbd", s + 1)
                    up("kt_sb", s + 1)
                    up("u_sb", s + 1)
                    for n, lhs, src in ((3, ktb, 2), (4, mbd, 1)):
                        for b in range(B):
                            last = mm(X[:, 64 * n + DH * b:64 * n + DH * b + DH], lhs[:, s % 2, b, :], usm[:, s % 2, src, DH * b:DH * b + DH], start=True, stop=True)
                    fin("ds_ps", last)

                def wo_():
                    up("og")
                    fin("wo_ps", to_tokens(0, kn, wo, "wo"))

                return {"turn1": turn1, "rot": rot, "unrot": unrot, "cond": cond, "proj": proj, "db": db, "sum": sum_, "decay": decay, "grow": grow,
                        "raw": raw, "old": old, "u": u_, "new": new, "wo": wo_}

            def second(j):
                def up(name, k=1):
                    pe.wait_ge(ev[name].sem, ev[name].at(j, k))

                def fin(name, ins):
                    ins.then_inc(ev[name].sem, 1)

                def turned(k):
                    up("turn_a", k)
                    up("turn_v", k)

                def turn2():
                    up("normed", 1)
                    fin("turn_ps", transposes(n2, 4))
                    turned(1)
                    for n in range(2):
                        last = over_k(bank[6 + n][:, :], lambda k: wq[:, k, n * P:n * P + P], lambda k: n2T[:, k, :])
                    fin("qx_ps", last)

                def sc(u):
                    b, hc = u // 2, u % 2
                    up("psub", u) if u else up("qx_sb")
                    for f in range(2):
                        last = mm(bank[4 + f][:, :], qx[64 * hc:64 * hc + 64, f, b * TB:b * TB + TB], kbx[64 * hc:64 * hc + 64, f, b, :], start=True, stop=True)
                    fin("sc_ps", last)

                def pt(u):
                    b, hc = u // 2, u % 2
                    up("pexp", u + 1)
                    for n in range(2):
                        if u or n:
                            up("pt_sb", 2 * u + n)
                        for h in range(4):
                            last = nc.tensor.transpose(bank[6][:, h * P:h * P + P], prob[:, 4 * n + h, :, :].rearrange("p f n -> p (f n)"), ident)
                        fin("pt_ps", last)
                        if n == 0 and u < 7:
                            sc(u + 1)
                    if u:
                        up("a_sb", u)
                    for n in range(2):
                        up("pt_sb", 2 * u + n + 1)
                        for h in range(4 * n, 4 * n + 4):
                            last = mm(bank[7][:, 34 * h:34 * h + 34], probT[:, h, :], vx[:, b, 8 * hc + h, :], start=True, stop=True)
                    fin("pv_ps", last)

                def anorm():
                    up("normed", 2)
                    fin("turn_ps", transposes(ax.rearrange("p b h v -> p b (h v)"), 4))

                def wp_():
                    turned(2)
                    fin("wp_ps", to_tokens(6, n2T, wp, "xp"))

                def turn4():
                    up("normed", 3)
                    fin("turn_ps", transposes(n2, 4))

                def pw_():
                    up("dconv")
                    for n in range(2):
                        last = over_k(bank[6 + n][:, :], lambda k: pw[:, k, n * P:n * P + P], lambda k: dcv[:, k, :])
                    fin("pw_ps", last)

                def router():
                    up("x1T")
                    for b in range(B):
                        dst = bank[4][:, b * NE:b * NE + NE]
                        for k in range(KC):
                            mm(dst, x1T[:, k, b * TB:b * TB + TB], rw_w[:, k, :], start=k == 0, stop=False)
                        last = bias(dst, "router")
                    fin("lgt_ps", last)

                def moe(u):
                    b, ep = u // 4, u % 4
                    if u == 3:
                        up("top")
                    if u >= 4:
                        up("moe_act", u - 3)
                    dst = bank[4 + (u + 1) % 4][:, :]
                    for k in range(KC):
                        mm(dst, x1T[:, k, b * TB:b * TB + TB], ew[:, k, ep * 512:ep * 512 + 512], start=k == 0, stop=False)
                    fin("moe_ps", bias(dst, "e", ep * 512, ep * 512 + 512))

                def turn5():
                    up("moe_acc", 16)
                    fin("turn_ps", transposes(comb, 4))

                def mo():
                    turned(4)
                    for b in range(B):
                        dst = bank[6 + b // 2][:, (b % 2) * D:(b % 2) * D + D]
                        for k in range(KC):
                            mm(dst, combT[:, k, b * TB:b * TB + TB], ow[:, k, :], start=k == 0, stop=False)
                        for k in range(KC):
                            mm(dst[:, k * P:k * P + P], x1T[:, k, b * TB:b * TB + TB], ident, start=False, stop=False)
                        last = bias(dst, "out")
                    fin("mo_ps", last)

                def turn6():
                    up("hn")
                    fin("turn_ps", transposes(hx, 4))

                def ffn():
                    turned(5)
                    fin("ffd_ps", over_k(bank[6][0:HID, :], lambda k: ffd[:, k, :], lambda k: hTT[:, k, :]))
                    up("gelu")
                    for b in range(B):
                        dst = bank[4 + b // 2][:, (b % 2) * D:(b % 2) * D + D]
                        mm(dst, gT[:, b * TB:b * TB + TB], ffu, start=True, stop=False)
                        last = bias(dst, "up")
                    fin("ffu_ps", last)

                return {"turn2": turn2, "sc": sc, "pt": pt, "anorm": anorm, "wp": wp_, "turn4": turn4, "pw": pw_, "router": router, "moe": moe,
                        "turn5": turn5, "mo": mo, "turn6": turn6, "ffn": ffn}

            turns(pe, first, second)


def layout(v):
    import numpy as np

    def chunks(w):
        return np.concatenate([w[:P], w[P:]], axis=1)

    def both(w):
        return w.reshape(KC, P).T

    reim = np.concatenate([np.arange(0, P, 2), np.arange(1, P, 2)])
    imre = np.concatenate([np.arange(1, P, 2), np.arange(0, P, 2)])
    zeros = lambda *s: np.zeros(s, np.float32)
    cin = v["L0_attn_cond_in_W"]
    dW = v["L0_attn_delta_W"][reim]
    cW, cb = v["L0_attn_ctrl_W"], v["L0_attn_ctrl_b"]
    dec, bet, gate = slice(768, 784), slice(784, 800), slice(800, 1056)
    rep = lambda a: np.repeat(a, DH, axis=-1)
    ctrl = np.concatenate([cW[:, :768], cW[:, gate], rep(cW[:, bet]), cW[:, dec], cW[:, bet]], axis=1)
    ew = v["L0_ffn_expert_w"].transpose(2, 0, 1).reshape(D, NE * D)
    parts = {
        "cin": chunks(np.concatenate([cin[:, reim], cin[:, imre]], axis=1)),
        "dw": np.concatenate([dW[:, :768], rep(dW[:, 768:784]), zeros(P, 16), dW[:, 768:784]], axis=1),
        "ctrl": chunks(ctrl), "wo": chunks(v["L0_attn_out_proj_W"].T), "wq": chunks(v["L0_xattn_Wq"].T),
        "wp": chunks(v["L0_xattn_Wp"].T), "pw": chunks(v["L0_ffn_pw_w"].T), "rw": chunks(v["L0_ffn_router_w"].T),
        "ew": chunks(ew), "ow": chunks(v["L0_ffn_out_w"].T), "normw": np.broadcast_to(v["L0_ffn_norm_w"], (P, D)),
        "ffd": chunks(v["L0_ffn_ff_down_w"].T), "ffu": np.concatenate([v["L0_ffn_ff_up_w"].T, zeros(HID, D)], axis=0)}
    weights = np.concatenate([parts[n] for n, _ in WEIGHTS], axis=1)

    p = np.arange(P)
    hp, tp = p // CH, p % CH
    f = lambda a: np.asarray(a, np.float32)
    same_t = tp[:, None] == tp[None, :]
    con = {
        "ident": f(np.eye(P)), "swap": f(np.eye(P)[np.concatenate([p[64:], p[:64]])]), "ones": f(np.ones((P, P))),
        "bones": f(hp[:, None] == hp[None, :]), "tri": -f(tp[:, None] <= tp[None, :]), "negones": -f(np.ones((P, P))),
        "delta": f(same_t), "triblk": -f((hp[:, None] == hp[None, :]) & (tp[:, None] <= tp[None, :])),
        "bd": f(hp[:, None] == np.arange(HG)), "mc": f(hp[:, None] == np.arange(NC)),
        "neg": f(np.where(np.arange(CH)[None, :] >= tp[:, None], 0.0, -1e30)), "hh": f((p % 64 // 8)[:, None] == np.arange(8)),
        "half": f((p // 64)[:, None] == np.arange(2)), "iota": f(np.broadcast_to(np.arange(NE), (P, NE))),
        "sgn": f(np.where(p < 64, 1.0, -1.0))[:, None], "dup": f((hp % 2)[:, None] == np.arange(2))}
    consts = np.concatenate([con[n] for n, _ in CONSTS], axis=1)

    conv = np.concatenate([v[f"L0_attn_{n}_conv_w"].reshape(KC, P, 4).transpose(1, 0, 2).reshape(P, 8) for n in "qkv"], axis=1)
    col = {
        "bproj": np.concatenate([cb[:768].reshape(6, P).T, both(cb[gate]), both(rep(cb[bet]))], axis=1),
        "conv": conv, "theta": np.tile(v["L0_attn_rot_theta"], 2)[:, None], "condnorm": v["L0_attn_cond_norm_w"][reim][:, None],
        "outnorm": np.tile(v["L0_attn_out_norm_w"], 8)[:, None], "subln": np.tile(v["L0_xattn_subln_w"], 8)[:, None],
        "pwb": both(v["L0_ffn_pw_b"]), "dwk": v["L0_ffn_dw_kernel"][:, 0, :].reshape(KC, P, 3).transpose(1, 0, 2).reshape(P, 6),
        "dwb": both(v["L0_ffn_dw_bias"]), "fdb": np.concatenate([v["L0_ffn_ff_down_b"], zeros(HID)])[:, None],
        "lam": np.broadcast_to(np.concatenate([v[f"L0_xattn_{n}"] for n in ("lq1", "lk1", "lq2", "lk2")]), (P, 32))}
    cols = np.concatenate([col[n] for n, _ in COLUMNS], axis=1)

    ramp = np.concatenate([v["L0_attn_qkv_ramp_logit"].reshape(768), rep(v["L0_attn_beta_ramp_logit"]), zeros(16), v["L0_attn_beta_ramp_logit"]])
    cT = v["ctx_1024"].transpose(2, 0, 1)
    scr = {
        "ramp": np.broadcast_to(ramp, (P, 1056)), "wk": chunks(v["L0_xattn_Wk"].T), "wv": chunks(v["L0_xattn_Wv"].T),
        "ctx": chunks(cT.reshape(D, B * NK)), "ctxd": chunks(np.concatenate([cT, cT], axis=2).reshape(D, B * 2 * NK))}
    scratch = np.concatenate([scr[n] for n, _ in SCRATCH], axis=1)

    bia = {"e": v["L0_ffn_expert_b"].reshape(-1), "out": v["L0_ffn_out_b"], "wo": v["L0_attn_out_proj_b"], "xp": v["L0_xattn_bp"],
           "up": v["L0_ffn_ff_up_b"], "router": v["L0_ffn_router_b"], "db": np.concatenate([cb[dec], cb[bet]])}
    biases = np.concatenate([bia[n] for n, _ in BIASES])[None, :]
    teye = f(np.tile(np.eye(CH).reshape(1, CH * CH), (P, 4)))
    return {"in_x": v["x"], "in_weights": weights, "in_consts": consts, "in_cols": cols, "in_scratch": scratch,
            "in_biases": biases, "in_teye": teye}


def kernel(**inputs):
    import numpy as np
    import concourse.bacc as bacc
    from concourse.bass_utils import run_bass_kernel_spmd as run

    nc = bacc.Bacc("TRN2", target_bir_lowering=False, num_devices=1)
    arrays = {n: np.ascontiguousarray(a) for n, a in layout({n: np.asarray(a) for n, a in inputs.items()}).items()}
    args = [nc.dram_tensor(n, a.shape, F32, kind="ExternalInput").ap() for n, a in arrays.items()]
    out = nc.dram_tensor("out_0", (B, S, D), F32, kind="ExternalOutput").ap()
    build(nc, args[0], out, *args[1:])
    r = run(nc, [arrays], core_ids=[0])
    return r.results[0]["out_0"]
```
